# Optimizing a Trainium2 kernel written in Bass

```python
import numpy as np
import jax
import jax.numpy as jnp

def _softmax(x, axis=-1):
    return jax.nn.softmax(x, axis=axis)

def _gelu(x):
    return jax.nn.gelu(x, approximate=True)

def _silu(x):
    return jax.nn.silu(x)

def _sigmoid(x):
    return jax.nn.sigmoid(x)

def _layernorm(x, axis=-1, eps=1e-05):
    m = jnp.mean(x, axis=axis, keepdims=True)
    v = jnp.var(x, axis=axis, keepdims=True)
    return (x - m) / jnp.sqrt(v + eps)

def _scatter_add(tgt, idx, src, axis=0):
    return tgt.at[idx].add(src)

def _segment_sum(src, seg, n):
    return jax.ops.segment_sum(src, seg, n)
kernel_name = 'mk_flamingo_gated_d1_seqx_r8_78bc29'

def setup_inputs(seed: int=0):
    np.random.seed(seed)
    _w = jnp.asarray

    def _rec_inputs():
        import jax
        import jax.numpy as jnp
        _rk = jax.random.key(seed)
        x = -0.000125 + 0.9999 * jax.random.normal(jax.random.fold_in(_rk, 1), (4, 512, 128), jnp.float32)
        _lenS = 512 - jax.random.randint(jax.random.fold_in(_rk, 7), (4,), 0, max(1, 512 // 4) + 1, jnp.int32)
        _lenS2 = 77 - jax.random.randint(jax.random.fold_in(_rk, 8), (4,), 0, max(1, 77 // 4) + 1, jnp.int32)
        _ctx_768P = jax.random.normal(jax.random.fold_in(_rk, 11), (4, 16, 96), jnp.float32)
        _ctx_768c = jax.random.dirichlet(jax.random.fold_in(_rk, 511), 0.3 * jnp.ones((16,), jnp.float32), (4, 77))
        _ctx_768t = jnp.einsum('bsk,bkd->bsd', _ctx_768c, _ctx_768P)
        _ctx_768t = _ctx_768t * jax.lax.rsqrt(jnp.mean(jnp.square(_ctx_768t)) + 1e-12) * 0.953939
        ctx_768 = 0.00272024 + 0.999456 * (_ctx_768t + 0.3 * jax.random.normal(jax.random.fold_in(_rk, 611), (4, 77, 96), jnp.float32))
        _g = jax.random.normal(jax.random.fold_in(_rk, 9001), (2, 1), jnp.float32)
        _g = jnp.sign(_g) * jnp.maximum(jnp.abs(_g), 1.0) + (_g == 0) * 1.0
        g_xattn = _g[0]
        g_ffn = _g[1]
        return (x, ctx_768, g_xattn, g_ffn)
    x, ctx_768, g_xattn, g_ffn = _rec_inputs()

    def _L0_xattn_setup():
        import jax, jax.numpy as jnp
        import numpy as np
        QUERY_DIM = 128
        CONTEXT_DIM = 96
        HEADS = 8
        DIM_HEAD = 64
        INNER = HEADS * DIM_HEAD
        key = jax.random.key(seed)
        ks = jax.random.split(key, 7)
        B, S, L = (8, 512, 77)
        x = jax.random.normal(ks[0], (B, S, QUERY_DIM), dtype=jnp.float32)
        context = jax.random.normal(ks[1], (B, L, CONTEXT_DIM), dtype=jnp.float32)
        Wq = jax.random.normal(ks[2], (QUERY_DIM, INNER), dtype=jnp.float32) * QUERY_DIM ** (-0.5)
        Wk = jax.random.normal(ks[3], (CONTEXT_DIM, INNER), dtype=jnp.float32) * CONTEXT_DIM ** (-0.5)
        Wv = jax.random.normal(ks[4], (CONTEXT_DIM, INNER), dtype=jnp.float32) * CONTEXT_DIM ** (-0.5)
        Wo = jax.random.normal(ks[5], (INNER, QUERY_DIM), dtype=jnp.float32) * INNER ** (-0.5)
        bo = jax.random.normal(ks[6], (QUERY_DIM,), dtype=jnp.float32) * 0.01
        return {'x': x, 'context': context, 'Wq': Wq, 'Wk': Wk, 'Wv': Wv, 'Wo': Wo, 'bo': bo}
    _L0_xattn_all = _L0_xattn_setup()
    _L0_xattn_in = {k: v for k, v in _L0_xattn_all.items() if k in ('Wq', 'Wk', 'Wv', 'Wo', 'bo')}
    del _L0_xattn_all

    def _L0_ffn_setup():
        import jax, jax.numpy as jnp
        import numpy as np
        B, S, D, E, F = (2, 256, 128, 8, 512)
        key = jax.random.key(seed)
        ks = jax.random.split(key, 4)
        return {'hidden_states': jax.random.normal(ks[0], (B, S, D), dtype=jnp.float32), 'Wr': jax.random.normal(ks[1], (D, E), dtype=jnp.float32) * (1.0 / np.sqrt(D)), 'W1': jax.random.normal(ks[2], (E, D, F), dtype=jnp.float32) * (1.0 / np.sqrt(D)), 'b1': jnp.zeros((E, F), dtype=jnp.float32), 'W2': jax.random.normal(ks[3], (E, F, D), dtype=jnp.float32) * (1.0 / np.sqrt(F)), 'b2': jnp.zeros((E, D), dtype=jnp.float32)}
    _L0_ffn_all = _L0_ffn_setup()
    _L0_ffn_in = {k: v for k, v in _L0_ffn_all.items() if k in ('Wr', 'W1', 'b1', 'W2', 'b2')}
    del _L0_ffn_all
    return {'x': x, 'ctx_768': ctx_768, 'g_xattn': g_xattn, 'g_ffn': g_ffn, 'L0_xattn_Wq': _L0_xattn_in['Wq'], 'L0_xattn_Wk': _L0_xattn_in['Wk'], 'L0_xattn_Wv': _L0_xattn_in['Wv'], 'L0_xattn_Wo': _L0_xattn_in['Wo'], 'L0_xattn_bo': _L0_xattn_in['bo'], 'L0_ffn_Wr': _L0_ffn_in['Wr'], 'L0_ffn_W1': _L0_ffn_in['W1'], 'L0_ffn_b1': _L0_ffn_in['b1'], 'L0_ffn_W2': _L0_ffn_in['W2'], 'L0_ffn_b2': _L0_ffn_in['b2']}

def reference(x, ctx_768, g_xattn, g_ffn, L0_xattn_Wq, L0_xattn_Wk, L0_xattn_Wv, L0_xattn_Wo, L0_xattn_bo, L0_ffn_Wr, L0_ffn_W1, L0_ffn_b1, L0_ffn_W2, L0_ffn_b2):
    import jax
    import jax.numpy as jnp

    def _L0_xattn_ref(x, context, Wq, Wk, Wv, Wo, bo):
        import jax, jax.numpy as jnp
        import numpy as np
        QUERY_DIM = 128
        CONTEXT_DIM = 96
        HEADS = 8
        DIM_HEAD = 64
        INNER = HEADS * DIM_HEAD
        B, S, _ = x.shape
        L = context.shape[1]
        scale = DIM_HEAD ** (-0.5)
        q = (x @ Wq).reshape(B, S, HEADS, DIM_HEAD).transpose(0, 2, 1, 3)
        k = (context @ Wk).reshape(B, L, HEADS, DIM_HEAD).transpose(0, 2, 1, 3)
        v = (context @ Wv).reshape(B, L, HEADS, DIM_HEAD).transpose(0, 2, 1, 3)
        attn = jnp.einsum('bhsd,bhld->bhsl', q, k) * scale
        attn = jax.nn.softmax(attn, axis=-1)
        out = jnp.einsum('bhsl,bhld->bhsd', attn, v)
        out = out.transpose(0, 2, 1, 3).reshape(B, S, INNER)
        return out @ Wo + bo

    def _L0_ffn_ref(hidden_states, Wr, W1, b1, W2, b2):
        import jax, jax.numpy as jnp
        import numpy as np
        B, S, D, E, F = (2, 256, 128, 8, 512)
        b, s, d = hidden_states.shape
        e = Wr.shape[1]
        x = hidden_states.reshape(b * s, d)
        router_logits = x @ Wr
        router_probs = jax.nn.softmax(router_logits, axis=-1)
        expert_idx = jnp.argmax(router_probs, axis=-1)
        p_max = jnp.max(router_probs, axis=-1, keepdims=True)

        def expert_mlp(w1, bb1, w2, bb2):
            h = jax.nn.gelu(x @ w1 + bb1, approximate=False)
            return h @ w2 + bb2
        outs = jax.vmap(expert_mlp)(W1, b1, W2, b2)
        onehot = jax.nn.one_hot(expert_idx, e, dtype=x.dtype)
        next_states = jnp.einsum('te,etd->td', onehot, outs)
        out = p_max * next_states
        return out.reshape(b, s, d)
    x = x + jnp.tanh(g_xattn[0]) * _L0_xattn_ref(_layernorm(x, axis=-1), ctx_768, L0_xattn_Wq, L0_xattn_Wk, L0_xattn_Wv, L0_xattn_Wo, L0_xattn_bo)
    x = x + jnp.tanh(g_ffn[0]) * _L0_ffn_ref(_layernorm(x, axis=-1), L0_ffn_Wr, L0_ffn_W1, L0_ffn_b1, L0_ffn_W2, L0_ffn_b2)
    return x

_drawn_inputs = setup_inputs


def setup_inputs(seed=0):
    import zlib

    import numpy as np

    out = dict(_drawn_inputs(seed))
    spreads = {'L0_ffn_b1': (0.0, 0.354), 'L0_ffn_b2': (0.0, 0.1)}
    factors = {'L0_xattn_bo': 3.489}
    for name, (base, spread) in spreads.items():
        noise = np.random.default_rng([zlib.crc32(name.encode()), seed]).standard_normal(out[name].shape)
        drawn = base * np.exp(spread * noise) if base else spread * noise
        out[name] = jnp.asarray(drawn.astype(out[name].dtype))
    for name, factor in factors.items():
        out[name] = (out[name] * factor).astype(out[name].dtype)
    return out
```

```python
from contextlib import ExitStack

import concourse.bass as bass
from concourse import mybir

F32 = mybir.dt.float32
BF16 = mybir.dt.bfloat16
I32 = mybir.dt.int32
ALU = mybir.AluOpType
ACT = mybir.ActivationFunctionType
AX = mybir.AxisListType.X

P = 128
EPS = 1e-5


def flamingo_block(nc, x, ctx_768, g_xattn, g_ffn, Wq, Wk, Wv, Wo, bo, Wr, W1, b1, W2, b2, out):
    B, S, D = x.shape
    _, L, C = ctx_768.shape
    INNER = Wq.shape[1]
    DH = 64
    H = INNER // DH
    E, _, F = W1.shape
    T = B * S // P
    NPAIR = T // 2
    PAIRS_PER_BATCH = S // P // 2
    HC = INNER // P
    HPC = P // DH
    FC = F // P
    HL = H * L
    HALF = HL // 2
    NCH = -(-HL // P)
    LASTC = HL - (NCH - 1) * P
    BL = B * L
    SCALE = float(DH) ** -0.5
    NTOK = B * S
    REGION = NTOK
    NJ = T + E - 1
    ROW = D + 4
    MEAN, RSTD, GATE, TOKEN = D, D + 1, D + 2, D + 3
    NW = 4
    DROP = float(2 * NTOK)
    assert D == P and H % 2 == 0 and LASTC < P and 4 * P == 512

    x_rows = x.rearrange("b s d -> (b s) d")
    out_rows = out.rearrange("b s d -> (b s) d")
    x_tiles = x_rows.rearrange("(t p) d -> p t d", p=P)
    scratch = nc.dram_tensor("expert_rows", [E * REGION, ROW], F32, kind="Internal").ap()

    with ExitStack() as es:
        def sb(name, shape, dt=F32):
            return es.enter_context(nc.sbuf_tensor(name, shape, dt))

        def sem(name):
            return es.enter_context(nc.semaphore(name))

        ctx_sb = sb("ctx_sb", [L, B, C])
        ctxT = sb("ctxT", [C, BL])
        wq_sb = sb("wq_sb", [P, INNER])
        wqT = sb("wqT", [P, HC, P])
        wk_sb = sb("wk_sb", [C, INNER])
        wv_sb = sb("wv_sb", [C, INNER])
        wo_sb = sb("wo_sb", [P, HC, D])
        kT = sb("kT", [P, HC, BL])
        vT = sb("vT", [P, HC, BL])
        A = sb("A", [P, B * HL])
        vwT = sb("vwT", [P, B, HL])
        vw = sb("vw", [P, B, NCH, D])
        wr_sb = sb("wr_sb", [P, E])
        w2_sb = sb("w2_sb", [P, E * FC * D])
        b1_rows = sb("b1_rows", [E * FC, P])
        b1T = sb("b1T", [P, E * FC])
        b2_bc = sb("b2_bc", [P, E * D])
        gates = sb("gates", [P, 2])
        tg = sb("tg", [P, 2])
        bo_row = sb("bo_row", [1, D])
        bo4 = sb("bo4", [1, B, D])
        ident = sb("ident", [P, P])
        tri = sb("tri", [P, P], BF16)
        ones_bf = sb("ones_bf", [P, P], BF16)
        rev = sb("rev", [P, E])
        expert_no = sb("expert_no", [P, E])
        region_no = sb("region_no", [P, E])
        ones8 = sb("ones8", [P, E])
        tile_edge = sb("tile_edge", [P, T])
        tile_no = sb("tile_no", [P, NJ])
        part_no = sb("part_no", [P, 1])
        pad = sb("pad", [P, ROW])
        x_sb = sb("x_sb", [P, T, D])
        stats1 = sb("stats1", [P, T, 6])
        mv1 = sb("mv1", [P, T, 2])
        rstd1 = sb("rstd1", [P, T])
        xn = sb("xn", [P, 2, D])
        xnT = sb("xnT", [P, 2, P])
        negmax = sb("negmax", [P, 2, H])
        expsum = sb("expsum", [P, 2, H])
        rsum = sb("rsum", [P, 2, H])
        probs = sb("probs", [P, 2, HL + 1])
        probsT = sb("probsT", [P, 2, NCH, P])
        rows = sb("rows", [P, T, ROW])
        stats2 = sb("stats2", [P, 2, 6])
        mv2 = sb("mv2", [P, 2, 2])
        var2 = sb("var2", [P, 2])
        rstd2 = sb("rstd2", [P, 2])
        xn2 = sb("xn2", [P, 2, D])
        eps = sb("eps", [P, 2])
        minus_half = sb("minus_half", [P, T])
        xn2T = sb("xn2T", [P, 2, P])
        logits = sb("logits", [P, 2, E])
        neg_lmax = sb("neg_lmax", [P, 2])
        is_max = sb("is_max", [P, 2, E])
        first_max = sb("first_max", [P, 2])
        onehot = sb("onehot", [P, 2, E], BF16)
        running = sb("running", [P, T + 1, E], BF16)
        lexp = sb("lexp", [P, 2, E])
        lsum = sb("lsum", [P, 2])
        lrec = sb("lrec", [P, 2])
        place = sb("place", [P, 2, E])
        place_f = sb("place_f", [P, 2])
        place_i = sb("place_i", [P, 2], I32)
        payload = sb("payload", [P, 2, ROW])
        cnt = sb("cnt", [P, E])
        above = sb("above", [P, E, T])
        ntiles = sb("ntiles", [P, E])
        cum_in = sb("cum_in", [P, E])
        cum_ex = sb("cum_ex", [P, E])
        sel = sb("sel", [P, NJ, E])
        sel2 = sb("sel2", [P, NJ, E])
        picked = sb("picked", [P, 3, NJ, E])
        pick = sb("pick", [P, 3, NJ])
        wanted = sb("wanted", [P, NJ])
        last_start = sb("last_start", [P, NJ])
        start = sb("start", [P, NJ])
        low = sb("low", [P, NJ])
        high = sb("high", [P, NJ])
        row_f = sb("row_f", [P, NJ])
        row_i = sb("row_i", [P, NJ], I32)
        expert_i = sb("expert_i", [P, NJ], I32)
        drop = sb("drop", [P, NJ])
        erows = sb("erows", [P, NJ, ROW])
        exn = sb("exn", [P, 2, D])
        exT = sb("exT", [P, 2, P])
        w1_sb = sb("w1_sb", [P, NW, F])
        hbias = sb("hbias", [P, 2, FC, P])
        hid = sb("hid", [P, 2, FC, P])
        ybias = sb("ybias", [P, 2, D])
        eout = sb("eout", [P, NW, D])
        token_i = sb("token_i", [P, NW], I32)

        bank = es.enter_context(nc.psum_tensor("bank", [P, 8, 512], F32))
        PT0, PT1, ATT, MISC = 4, 5, 6, 7

        ctx_in, wq_in, wk_in, wv_in, wo_in = (sem(n) for n in ("ctx_in", "wq_in", "wk_in", "wv_in", "wo_in"))
        x_in = [sem(f"x_in{b}") for b in range(B)]
        gates_in, wr_in, bo_in, b1_in, b2_in, w2_in = (
            sem(n) for n in ("gates_in", "wr_in", "bo_in", "b1_in", "b2_in", "w2_in"))
        pads_out, bias_row_in = sem("pads_out"), sem("bias_row_in")
        memsets, consts = sem("memsets"), sem("consts")
        setup_ready, setup_act, setup_dve = sem("setup_ready"), sem("setup_act"), sem("setup_dve")
        tanh_ready, bo4_ready = sem("tanh_ready"), sem("bo4_ready")
        ln1_step, rstd1_ready = sem("ln1_step"), sem("rstd1_ready")
        xn_ready, xT_ready, xnT_ready = sem("xn_ready"), sem("xT_ready"), sem("xnT_ready")
        scores_ready, max_ready, exp_ready = sem("scores_ready"), sem("max_ready"), sem("exp_ready")
        rsum_ready, probs_ready = sem("rsum_ready"), sem("probs_ready")
        pT_ready, probsT_ready = sem("pT_ready"), sem("probsT_ready")
        attn_ready, resid_ready = sem("attn_ready"), sem("resid_ready")
        stats2_ready = [sem("stats2_ready0"), sem("stats2_ready1")]
        mv2_ready, var2_ready, rstd2_ready, mv2_used = (sem(n) for n in ("mv2_ready", "var2_ready", "rstd2_ready", "mv2_used"))
        xn2_ready, x2T_ready, xn2T_ready = sem("xn2_ready"), sem("x2T_ready"), sem("xn2T_ready")
        logits_ready, logits_copied, lexp_ready = sem("logits_ready"), sem("logits_copied"), sem("lexp_ready")
        router_step, running_step, place_step = sem("router_step"), sem("running_step"), sem("place_step")
        stats_in_rows = sem("stats_in_rows")
        rank_ready, rank_read, place_ready = sem("rank_ready"), sem("rank_read"), sem("place_ready")
        neg_lmax_ready, payload_copied = sem("neg_lmax_ready"), sem("payload_copied")
        scattered = [sem("scattered0"), sem("scattered1")]
        cnt_ready, plan_step = sem("cnt_ready"), sem("plan_step")
        erows_in = [sem(f"erows_in{k}") for k in range(NW)]
        w1_in = [sem(f"w1_in{k}") for k in range(NW)]
        exn_ready, exT_psum, exT_ready = sem("exn_ready"), sem("exT_psum"), sem("exT_ready")
        h_ready, hbias_ready, hid_ready = sem("h_ready"), sem("hbias_ready"), sem("hid_ready")
        y_ready, ybias_ready = sem("y_ready"), sem("ybias_ready")
        eout_ready = [sem(f"eout_ready{k}") for k in range(NW)]
        token_ready = [sem(f"token_ready{k}") for k in range(NW)]
        stored = [sem(f"stored{k}") for k in range(NW)]

        k_side = [("ctxT", 0, 0, "dve"), ("wqT", 0, 1, "act")]
        k_side += [("kT", c, 2 + c, ("dve", "act")[c % 2]) for c in range(HC)]
        k_side += [("A", h, (6 + h) % 8, ("dve", "act")[h % 2]) for h in range(H)]
        v_side = [("vT", c, 4 + c, "dve") for c in range(HC)]
        v_side += [("vwT", h, 4 + h % 4, "dve") for h in range(H)]
        v_side += [("vw", b, 4 + b, "dve") for b in range(B)]
        v_side += [("vw_last", 0, 4, "dve"), ("b1T", 0, 5, "dve")]
        groups = k_side + v_side

        def emptied(eng, n):
            who = groups[n][3]
            count = sum(1 for g in groups[:n + 1] if g[3] == who)
            eng.wait_ge(setup_act if who == "act" else setup_dve, count)

        def group(what, index):
            return next(n for n, g in enumerate(groups) if g[:2] == (what, index))

        def last_in_bank(b, before):
            return max((n for n, g in enumerate(groups[:before]) if g[2] == b), default=None)

        def empty(eng, n, src_bank, what, i):
            act = eng is nc.scalar

            def copy(dst, src, scale=None):
                if act:
                    return nc.scalar.activation(dst, src, ACT.Copy, scale=1.0 if scale is None else scale)
                if scale is None:
                    return nc.vector.tensor_copy(dst, src)
                return nc.vector.tensor_scalar(dst, src, scale, None, ALU.mult)

            full = bank[:, src_bank, :]
            per_b = bank[:, src_bank, 0:BL].rearrange("p (b l) -> p b l", b=B)
            if what == "ctxT":
                return copy(ctxT[:, :], bank[0:C, src_bank, 0:BL])
            if what == "wqT":
                return copy(wqT[:, :, :].rearrange("p c d -> p (c d)"), full, SCALE)
            if what == "kT":
                return copy(kT[:, i, :], bank[:, src_bank, 0:BL])
            if what == "A":
                return copy(A[:, :].rearrange("p (b h l) -> p b h l", b=B, h=H)[:, :, i, :], per_b)
            if what == "vT":
                return copy(vT[:, i, :], bank[:, src_bank, 0:BL])
            if what == "vwT":
                return copy(vwT[:, :, i * L:(i + 1) * L], per_b, tg[:, 0:1])
            if what == "vw":
                return copy(vw[:, i, 0:NCH - 1, :].rearrange("p c d -> p (c d)"), full)
            if what == "vw_last":
                return copy(vw[0:LASTC, :, NCH - 1, :],
                            bank[0:LASTC, src_bank, :].rearrange("p (b d) -> p b d", b=B))
            return copy(b1T[:, :], bank[:, src_bank, 0:E * FC])

        def fixed_wait(eng):
            eng.wait_ge(consts, 1)

        block = es.enter_context(nc.Block())

        @block.sync
        def _(sp):
            sp.dma_start(ctx_sb[:, :, :], ctx_768.rearrange("b l c -> l b c")).then_inc(ctx_in, 16)
            sp.dma_start(wk_sb[:, :], Wk).then_inc(wk_in, 16)
            for b in range(B):
                per = S // P
                sp.dma_start(x_sb[:, b * per:(b + 1) * per, :], x_tiles[:, b * per:(b + 1) * per, :]).then_inc(x_in[b], 16)
            sp.dma_start(b2_bc[:, :], b2.rearrange("(o e) d -> o (e d)", o=1).partition_broadcast(P)).then_inc(b2_in, 16)
            sp.dma_start(w2_sb[:, :].rearrange("p (e c d) -> p e c d", e=E, c=FC),
                         W2.rearrange("e (c p) d -> p e c d", p=P)).then_inc(w2_in, 16)
            sp.wait_ge(memsets, 4)
            for e in range(E):
                sp.dma_start(scratch[e * REGION:e * REGION + P, :], pad[:, :]).then_inc(pads_out, 16)
            sp.wait_ge(bo4_ready, 1)
            sp.dma_start(vw[LASTC:LASTC + 1, :, NCH - 1, :], bo4[:, :, :]).then_inc(bias_row_in, 16)

            def load_tile(j, k):
                first_row = sp.value_load(row_i[0:1, bass.ds(j, 1)], min_val=0, max_val=E * REGION - P)
                sp.dma_start(erows[:, bass.ds(j, 1), :].rearrange("p o w -> p (o w)"),
                             scratch[bass.ds(first_row, P), :]).then_inc(erows_in[k], 16)
                expert = sp.value_load(expert_i[0:1, bass.ds(j, 1)], min_val=0, max_val=E - 1)
                sp.dma_start(w1_sb[:, k, :], W1[bass.ds(expert, 1), :, :].rearrange("o p f -> (o p) f"))\
                    .then_inc(w1_in[k], 16)

            sp.wait_ge(plan_step, PLAN_STEPS)
            for k in (0, 1):
                sp.wait_ge(scattered[k], 16 * NPAIR)
            for j in range(NW):
                load_tile(j, j)
            with sp.Fori(0, NJ - NW - (NJ - NW) % NW, NW) as j0:
                for k in range(NW):
                    sp.wait_ge(h_ready, j0 + k + 1)
                    load_tile(j0 + NW + k, k)
            for j in range(NJ - (NJ - NW) % NW, NJ):
                sp.wait_ge(h_ready, j - NW + 1)
                load_tile(j, j % NW)

        @block.gpsimd
        def _(pool):
            nc.gpsimd.memset(ident[:, :], 0.0).then_inc(memsets, 1)
            nc.gpsimd.memset(tri[:, :], 1.0).then_inc(memsets, 1)
            nc.gpsimd.memset(ones_bf[:, :], 1.0).then_inc(memsets, 1)
            nc.gpsimd.memset(pad[:, :], 0.0).then_inc(memsets, 1)
            pool.wait_ge(memsets, 2)
            nc.gpsimd.affine_select(out=ident[:, :], in_=ident[:, :], compare_op=ALU.not_equal, fill=1.0,
                                    base=0, pattern=[[-1, P]], channel_multiplier=1).then_inc(consts, 1)
            nc.gpsimd.affine_select(out=tri[:, :], in_=tri[:, :], compare_op=ALU.is_gt, fill=0.0,
                                    base=0, pattern=[[1, P]], channel_multiplier=-1).then_inc(consts, 1)

            def count_up(dst, step, n, base=0, per_partition=0):
                nc.gpsimd.iota(dst, [[step, n]], base=base, channel_multiplier=per_partition,
                               allow_small_or_imprecise_dtypes=True).then_inc(consts, 1)

            count_up(rev[:, :], -1, E, base=E)
            count_up(expert_no[:, :], 1, E)
            count_up(region_no[:, :], REGION, E)
            count_up(tile_edge[:, :], P, T)
            count_up(tile_no[:, :], 1, NJ)
            count_up(part_no[:, :], 0, 1, per_partition=1)
            count_up(rows[:, :, TOKEN:TOKEN + 1].rearrange("p t o -> p (t o)"), P, T, per_partition=1)
            nc.gpsimd.memset(ones8[:, :], 1.0).then_inc(consts, 1)
            nc.gpsimd.memset(running[:, 0, :], 0.0).then_inc(consts, 1)
            nc.gpsimd.memset(probs[:, :, HL:HL + 1], 1.0).then_inc(consts, 1)

            def normalise(t, s):
                pool.wait_ge(rsum_ready, t + 1)
                v = probs[:, s, 0:HL].rearrange("p (h l) -> p h l", h=H)
                nc.gpsimd.tensor_tensor(v, v, rsum[:, s, :].unsqueeze(2).to_broadcast([P, H, L]), ALU.mult)\
                    .then_inc(probs_ready, 1)

            def scatter(r, first):
                pool.wait_ge(place_ready, r + 1)
                pool.wait_ge(stats_in_rows, r + 1)
                pool.wait_ge(mv2_used, r + 1)
                for i in range(2):
                    if not first:
                        pool.wait_ge(scattered[i], 16 * r)
                    nc.gpsimd.tensor_copy(payload[:, i, :],
                                          rows[:, bass.ds(2 * r + i, 1), :].rearrange("p o w -> p (o w)"))\
                        .then_inc(payload_copied, 1)
                for i in range(2):
                    fixed_wait(pool)
                    pool.wait_ge(payload_copied, 2 * r + i + 1)
                    nc.gpsimd.indirect_dma_start(scratch, bass.IndirectOffsetOnAxis(place_i[:, i:i + 1], 0),
                                                 payload[:, i, :], None,
                                                 bounds_check=E * REGION - 1, oob_is_err=False)\
                        .then_inc(scattered[i], 16)

            def invert_std(r, first=False):
                pool.wait_ge(mv2_ready, 2 * r + 2)
                nc.gpsimd.tensor_tensor(var2[:, :].unsqueeze(2), mv2[:, :, 1:2], eps[:, :].unsqueeze(2), ALU.add)\
                    .then_inc(var2_ready, 1)
                pool.wait_ge(var2_ready, r + 1)
                if not first:
                    pool.wait_ge(xn2_ready, r)
                nc.gpsimd.tensor_tensor(rstd2[:, :], var2[:, :], minus_half[:, 0:2], ALU.pow).then_inc(rstd2_ready, 1)
                pool.wait_ge(rstd2_ready, r + 1)
                nc.gpsimd.tensor_copy(rows[:, bass.ds(2 * r, 2), RSTD:RSTD + 1], rstd2[:, :].unsqueeze(2)).then_inc(stats_in_rows, 1)
                nc.gpsimd.tensor_copy(rows[:, bass.ds(2 * r, 2), MEAN:MEAN + 1], mv2[:, :, 0:1]).then_inc(mv2_used, 1)

            def pair(j, first=False, last=False, early=False):
                if not first:
                    invert_std(j - 1, early)
                normalise(2 * j + 1, 1)
                if not last:
                    normalise(2 * j + 2, 0)
                if not first:
                    scatter(j - 1, early)

            nc.gpsimd.memset(minus_half[:, :], -0.5).then_inc(consts, 1)
            nc.gpsimd.memset(eps[:, :], EPS).then_inc(consts, 1)
            pool.wait_ge(consts, CONSTS)
            pool.wait_ge(ln1_step, T + 2)
            nc.gpsimd.tensor_tensor(rstd1[:, :], rstd1[:, :], minus_half[:, :], ALU.pow).then_inc(rstd1_ready, 1)
            normalise(0, 0)
            pool.wait_ge(pads_out, 16 * E)
            pair(0, first=True)
            pair(1, early=True)
            with pool.Fori(2, NPAIR - 1) as j:
                pair(j)
            pair(NPAIR - 1, last=True)
            invert_std(NPAIR - 1)
            scatter(NPAIR - 1, False)

            def store(k, uses):
                fixed_wait(pool)
                pool.wait_ge(eout_ready[k], uses)
                pool.wait_ge(token_ready[k], uses)
                nc.gpsimd.indirect_dma_start(out_rows, bass.IndirectOffsetOnAxis(token_i[:, k:k + 1], 0),
                                             eout[:, k, :], None, bounds_check=NTOK - 1, oob_is_err=False)\
                    .then_inc(stored[k], 16)

            with pool.Fori(1, NJ // NW + 1) as uses:
                for k in range(NW):
                    store(k, uses)
            for k in range(NJ % NW):
                store(k, NJ // NW + 1)
            for k in range(NW):
                pool.wait_ge(stored[k], 16 * len(range(k, NJ, NW)))

        @block.scalar
        def _(act):
            act.dma_start(wq_sb[:, :], Wq).then_inc(wq_in, 16)
            act.dma_start(gates[:, 0:1], g_xattn.rearrange("(o g) -> o g", o=1).partition_broadcast(P)).then_inc(gates_in, 16)
            act.dma_start(gates[:, 1:2], g_ffn.rearrange("(o g) -> o g", o=1).partition_broadcast(P)).then_inc(gates_in, 16)
            act.dma_start(wv_sb[:, :], Wv).then_inc(wv_in, 16)
            act.dma_start(wo_sb[:, :, :], Wo.rearrange("(c p) d -> p c d", p=P)).then_inc(wo_in, 16)
            act.dma_start(bo_row[:, :], bo.rearrange("(o d) -> o d", o=1)).then_inc(bo_in, 16)
            act.dma_start(wr_sb[:, :], Wr).then_inc(wr_in, 16)
            act.dma_start(b1_rows[:, :], b1.rearrange("e (c p) -> (e c) p", p=P)).then_inc(b1_in, 16)

            for n, (what, i, b, who) in enumerate(groups):
                if who == "act":
                    act.wait_ge(setup_ready, n + 1)
                    empty(nc.scalar, n, b, what, i).then_inc(setup_act, 1)
            act.wait_ge(gates_in, 32)
            nc.scalar.activation(tg[:, :], gates[:, :], ACT.Tanh).then_inc(tanh_ready, 1)

            def exps(t, s, first=False):
                act.wait_ge(max_ready, t + 1)
                if not first:
                    act.wait_ge(pT_ready, t - 1)
                    act.wait_ge(rsum_ready, t - 1)
                for h in range(H):
                    src = bank[:, 2 * s + h // (H // 2), (h % (H // 2)) * L:(h % (H // 2) + 1) * L]
                    step = nc.scalar.activation(probs[:, s, h * L:(h + 1) * L], src, ACT.Exp,
                                                bias=negmax[:, s, h:h + 1], accum_out=expsum[:, s, h:h + 1])
                step.then_inc(exp_ready, 1)

            def copy_probsT(t, s, first=False):
                act.wait_ge(pT_ready, t + 1)
                if not first:
                    act.wait_ge(attn_ready, t - 1)
                nc.scalar.activation(probsT[:, s, 0:NCH - 1, :].rearrange("p c k -> p (c k)"),
                                     bank[:, PT0, :], ACT.Copy)
                nc.scalar.activation(probsT[0:LASTC + 1, s, NCH - 1, :], bank[0:LASTC + 1, PT1, 0:P], ACT.Copy)\
                    .then_inc(probsT_ready, 1)

            def router_exps(r):
                act.wait_ge(neg_lmax_ready, r + 1)
                for i in range(2):
                    step = nc.scalar.activation(lexp[:, i, :], logits[:, i, :], ACT.Exp,
                                                bias=neg_lmax[:, i:i + 1], accum_out=lsum[:, i:i + 1])
                step.then_inc(lexp_ready, 1)

            def pair(j, first=False, last=False):
                copy_probsT(2 * j, 0, first)
                exps(2 * j + 1, 1, first)
                copy_probsT(2 * j + 1, 1, first)
                if not last:
                    exps(2 * j + 2, 0)
                if not first:
                    router_exps(j - 1)

            exps(0, 0, True)
            pair(0, first=True)
            with act.Fori(1, NPAIR - 1) as j:
                pair(j)
            pair(NPAIR - 1, last=True)
            router_exps(NPAIR - 1)

            def gelu(j, s, first=False):
                act.wait_ge(hbias_ready, j + 1)
                if not first:
                    act.wait_ge(y_ready, j - 1)
                nc.scalar.activation(hid[:, s, :, :].rearrange("p c k -> p (c k)"),
                                     hbias[:, s, :, :].rearrange("p c k -> p (c k)"), ACT.Gelu)\
                    .then_inc(hid_ready, 1)

            gelu(0, 0, True)
            gelu(1, 1, True)
            with act.Fori(2, NJ - 1 - (NJ - 1) % 2, 2) as j:
                gelu(j, 0)
                gelu(j + 1, 1)
            for j in range(NJ - 1 - (NJ - 1) % 2, NJ):
                gelu(j, j % 2)

        @block.tensor
        def _(pe):
            pe.wait_ge(consts, 1)

            def setup(lo, hi):
                for n in range(lo, hi):
                    what, i, b, _ = groups[n]
                    if (prev := last_in_bank(b, n)) is not None:
                        emptied(pe, prev)
                    if what == "ctxT":
                        pe.wait_ge(ctx_in, 16)
                        for k in range(B):
                            step = nc.tensor.transpose(bank[0:C, b, k * L:(k + 1) * L], ctx_sb[:, k, :], ident[0:L, 0:L])
                    elif what == "wqT":
                        pe.wait_ge(wq_in, 16)
                        for c in range(HC):
                            step = nc.tensor.transpose(bank[:, b, c * P:(c + 1) * P], wq_sb[:, c * P:(c + 1) * P], ident[:, :])
                    elif what in ("kT", "vT"):
                        pe.wait_ge(wk_in if what == "kT" else wv_in, 16)
                        emptied(pe, group("ctxT", 0))
                        w = wk_sb if what == "kT" else wv_sb
                        step = nc.tensor.matmul(bank[:, b, 0:BL], w[:, i * P:(i + 1) * P], ctxT[:, :], start=True, stop=True)
                    elif what in ("A", "vwT"):
                        c, at = i // HPC, (i % HPC) * DH
                        emptied(pe, group("kT" if what == "A" else "vT", c))
                        if what == "A":
                            emptied(pe, group("wqT", 0))
                            w, m = wqT[at:at + DH, c, :], kT[at:at + DH, c, :]
                        else:
                            pe.wait_ge(wo_in, 16)
                            w, m = wo_sb[at:at + DH, c, :], vT[at:at + DH, c, :]
                        step = nc.tensor.matmul(bank[:, b, 0:BL], w, m, start=True, stop=True)
                    elif what == "vw":
                        emptied(pe, group("vwT", H - 1))
                        for c in range(NCH - 1):
                            step = nc.tensor.transpose(bank[:, b, c * P:(c + 1) * P], vwT[:, i, c * P:(c + 1) * P], ident[:, :])
                    elif what == "vw_last":
                        for k in range(B):
                            step = nc.tensor.transpose(bank[0:LASTC, b, k * P:(k + 1) * P], vwT[:, k, (NCH - 1) * P:HL], ident[:, :])
                    else:
                        pe.wait_ge(b1_in, 16)
                        step = nc.tensor.transpose(bank[:, b, 0:E * FC], b1_rows[:, :], ident[0:E * FC, 0:E * FC])
                    step.then_inc(setup_ready, 1)

            def transpose_x(j, first=False, second=False, third=False):
                pe.wait_ge(xn_ready, 2 * j + 2)
                if first:
                    emptied(pe, last_in_bank(MISC, len(k_side)))
                elif second:
                    emptied(pe, last_in_bank(MISC, len(groups)))
                elif third:
                    pe.wait_ge(xnT_ready, j)
                else:
                    pe.wait_ge(rank_read, j - 2)
                for i in range(2):
                    step = nc.tensor.transpose(bank[:, MISC, i * P:(i + 1) * P], xn[:, i, :], ident[:, :])
                step.then_inc(xT_ready, 1)

            def scores(t, s, batch, first=False):
                pe.wait_ge(xnT_ready, t // 2 + 1 if first else batch_pair_count(t, s))
                if first:
                    for b in (2 * s, 2 * s + 1):
                        emptied(pe, last_in_bank(b, len(k_side)))
                    emptied(pe, group("A", H - 1))
                    emptied(pe, group("A", H - 2))
                else:
                    pe.wait_ge(exp_ready, t - 1)
                for half in range(2):
                    step = nc.tensor.matmul(bank[:, 2 * s + half, 0:HALF], xnT[:, s, :],
                                            A[:, bass.ds(batch * HL + half * HALF, HALF)], start=True, stop=True)
                step.then_inc(scores_ready, 1)

            def batch_pair_count(t, s):
                return (t - s) // 2 + 1

            def transpose_probs(t, s, first=False):
                pe.wait_ge(probs_ready, t + 1)
                if first:
                    emptied(pe, last_in_bank(PT0, len(groups)))
                    emptied(pe, last_in_bank(PT1, len(groups)))
                else:
                    pe.wait_ge(probsT_ready, t)
                for c in range(NCH - 1):
                    nc.tensor.transpose(bank[:, PT0, c * P:(c + 1) * P], probs[:, s, c * P:(c + 1) * P], ident[:, :])
                nc.tensor.transpose(bank[0:LASTC + 1, PT1, 0:P], probs[:, s, (NCH - 1) * P:HL + 1], ident[:, :])\
                    .then_inc(pT_ready, 1)

            def attend(t, s, batch, first=False):
                pe.wait_ge(probsT_ready, t + 1)
                if first:
                    pe.wait_ge(bias_row_in, 16)
                    emptied(pe, last_in_bank(ATT, len(groups)))
                else:
                    pe.wait_ge(resid_ready, t)
                for c in range(NCH):
                    k = P if c < NCH - 1 else LASTC + 1
                    step = nc.tensor.matmul(bank[:, ATT, 0:D], probsT[0:k, s, c, :],
                                            vw[0:k, bass.ds(batch, 1), c, :].rearrange("p o d -> p (o d)"),
                                            start=c == 0, stop=c == NCH - 1)
                step.then_inc(attn_ready, 1)

            def transpose_x2(r, late=False):
                pe.wait_ge(xn2_ready, r + 1)
                if late:
                    pe.wait_ge(rank_read, r)
                else:
                    pe.wait_ge(xnT_ready, r + 3)
                for i in range(2):
                    step = nc.tensor.transpose(bank[:, MISC, i * P:(i + 1) * P], xn2[:, i, :], ident[:, :])
                step.then_inc(x2T_ready, 1)

            def router(r, first=False):
                pe.wait_ge(xn2T_ready, r + 1)
                if first:
                    pe.wait_ge(wr_in, 16)
                for i in range(2):
                    step = nc.tensor.matmul(bank[:, MISC, i * E:(i + 1) * E], xn2T[:, i, :], wr_sb[:, :], start=True, stop=True)
                step.then_inc(logits_ready, 1)

            def ranks(r):
                pe.wait_ge(router_step, 4 * r + 4)
                pe.wait_ge(running_step, 2 * r + 1)
                pe.wait_ge(logits_copied, r + 1)
                nc.tensor.matmul(bank[:, MISC, 0:2 * E], tri[:, :], onehot[:, :, :].rearrange("p i e -> p (i e)"),
                                 start=True, stop=False)
                nc.tensor.matmul(bank[:, MISC, 0:2 * E], ones_bf[:, :],
                                 running[:, bass.ds(2 * r, 2), :].rearrange("p i e -> p (i e)"),
                                 start=False, stop=True).then_inc(rank_ready, 1)

            def pair(j, batch, next_batch, first=False, last=False, second=False):
                if not last:
                    transpose_x(j + 1, second=first, third=second)
                transpose_probs(2 * j, 0, first)
                if not last:
                    scores(2 * j + 2, 0, next_batch)
                attend(2 * j, 0, batch, first)
                if not first:
                    transpose_x2(j - 1, last)
                transpose_probs(2 * j + 1, 1)
                if not first:
                    router(j - 1, second)
                if not last:
                    scores(2 * j + 3, 1, next_batch)
                if not first:
                    ranks(j - 1)
                attend(2 * j + 1, 1, batch)

            setup(0, len(k_side))
            transpose_x(0, first=True)
            scores(0, 0, 0, True)
            scores(1, 1, 0, True)
            pe.wait_ge(xnT_ready, 1)
            setup(len(k_side), len(groups))
            pair(0, 0, 0, first=True)
            pair(1, 0, 1, second=True)
            with pe.Fori(2, NPAIR - 1) as j:
                pair(j, j // PAIRS_PER_BATCH, (j + 1) // PAIRS_PER_BATCH)
            pair(NPAIR - 1, B - 1, B - 1, last=True)
            r = NPAIR - 1
            transpose_x2(r, True)
            router(r)
            ranks(r)
            pe.wait_ge(rank_read, NPAIR)
            nc.tensor.matmul(bank[:, MISC, 0:E], ones_bf[:, :], running[:, T, :], start=True, stop=True).then_inc(cnt_ready, 1)

            def transpose_rows(j, s, first=False):
                pe.wait_ge(exn_ready, j + 1)
                if not first:
                    pe.wait_ge(exT_ready, j - 1)
                nc.tensor.transpose(bank[:, s, 0:P], exn[:, s, :], ident[:, :]).then_inc(exT_psum, 1)

            def hidden(j, s, k, uses, first=False):
                pe.wait_ge(exT_ready, j + 1)
                pe.wait_ge(w1_in[k], 16 * uses)
                if not first:
                    pe.wait_ge(hbias_ready, j - 1)
                for c in range(FC):
                    step = nc.tensor.matmul(bank[:, 2 + s, c * P:(c + 1) * P], w1_sb[:, k, c * P:(c + 1) * P],
                                            exT[:, s, :], start=True, stop=True)
                step.then_inc(h_ready, 1)

            def outputs(j, s, first=False):
                expert = pe.value_load(expert_i[0:1, bass.ds(j, 1)], min_val=0, max_val=E - 1)
                pe.wait_ge(hid_ready, j + 1)
                if not first:
                    pe.wait_ge(ybias_ready, j - 1)
                for c in range(FC):
                    step = nc.tensor.matmul(bank[:, 4 + s, 0:D], hid[:, s, c, :],
                                            w2_sb[:, bass.ds(expert * (FC * D) + c * D, D)],
                                            start=c == 0, stop=c == FC - 1)
                step.then_inc(y_ready, 1)

            pe.wait_ge(w2_in, 16)
            pe.wait_ge(plan_step, PLAN_STEPS)
            transpose_rows(0, 0, True)
            transpose_rows(1, 1, True)
            hidden(0, 0, 0, 1, True)

            def slot(j, k, uses, first=False, second=False):
                after = (j + 2 < NJ, j + 1 < NJ) if isinstance(j, int) else (True, True)
                if after[0]:
                    transpose_rows(j + 2, k % 2)
                if after[1]:
                    hidden(j + 1, (k + 1) % 2, (k + 1) % NW, uses + (k + 1) // NW, first)
                outputs(j, k % 2, second)

            for j in range(NW):
                slot(j, j, 1, j < 1, j < 2)
            with pe.Fori(1, (NJ - 2) // NW) as q:
                for k in range(NW):
                    slot(NW * q + k, k, q + 1)
            for j in range((NJ - 2) // NW * NW, NJ):
                slot(j, j % NW, j // NW + 1)

        @block.vector
        def _(dve):
            for b in range(B):
                dve.wait_ge(x_in[b], 16)
            with dve.Fori(0, T) as t:
                nc.vector.bn_stats(stats1[:, bass.ds(t, 1), :].rearrange("p o s -> p (o s)"),
                                   x_sb[:, bass.ds(t, 1), :].rearrange("p o d -> p (o d)")).then_inc(ln1_step, 1)
            dve.wait_ge(ln1_step, T)
            for t in range(T):
                step = nc.vector.bn_aggr(mv1[:, t, :], stats1[:, t, :])
            step.then_inc(ln1_step, 1)
            dve.wait_ge(ln1_step, T + 1)
            nc.vector.tensor_scalar(rstd1[:, :].unsqueeze(2), mv1[:, :, 1:2], EPS, None, ALU.add).then_inc(ln1_step, 1)
            dve.wait_ge(rstd1_ready, 1)

            def normalise_x(j, first=False):
                if not first:
                    dve.wait_ge(xT_ready, j)
                for i in range(2):
                    nc.vector.tensor_scalar(xn[:, i, :], x_sb[:, bass.ds(2 * j + i, 1), :].rearrange("p o d -> p (o d)"),
                                            mv1[:, bass.ds(2 * j + i, 1), 0:1].rearrange("p o s -> p (o s)"),
                                            rstd1[:, bass.ds(2 * j + i, 1)],
                                            ALU.subtract, ALU.mult).then_inc(xn_ready, 1)

            def copy_xT(j, first=False):
                dve.wait_ge(xT_ready, j + 1)
                if not first:
                    dve.wait_ge(scores_ready, 2 * j)
                nc.vector.tensor_copy(xnT[:, :, :].rearrange("p i k -> p (i k)"), bank[:, MISC, 0:2 * P]).then_inc(xnT_ready, 1)

            def head_max(t, s, first=False):
                dve.wait_ge(scores_ready, t + 1)
                if not first:
                    dve.wait_ge(exp_ready, t - 1)
                nc.vector.tensor_reduce(negmax[:, s, :].rearrange("p (b h) -> p b h", b=2),
                                        bank[:, 2 * s:2 * s + 2, 0:HALF].rearrange("p b (h l) -> p b h l", l=L),
                                        AX, ALU.max, negate=True).then_inc(max_ready, 1)

            def invert_sums(t, s, first=False):
                dve.wait_ge(exp_ready, t + 1)
                if not first:
                    dve.wait_ge(probs_ready, t - 1)
                nc.vector.reciprocal(rsum[:, s, :], expsum[:, s, :]).then_inc(rsum_ready, 1)

            def residual(t, s, first=False):
                dve.wait_ge(attn_ready, t + 1)
                x2 = rows[:, bass.ds(t, 1), 0:D].rearrange("p o d -> p (o d)")
                nc.vector.tensor_tensor(x2, bank[:, ATT, 0:D],
                                        x_sb[:, bass.ds(t, 1), :].rearrange("p o d -> p (o d)"), ALU.add).then_inc(resid_ready, 1)
                fixed_wait(dve)
                dve.wait_ge(resid_ready, t + 1)
                nc.vector.bn_stats(stats2[:, s, :], x2).then_inc(stats2_ready[s], 1)

            def aggregate_x2(r, count):
                for i in range(2):
                    fixed_wait(dve)
                    dve.wait_ge(stats2_ready[i], count)
                    nc.vector.bn_aggr(mv2[:, i, :], stats2[:, i, :]).then_inc(mv2_ready, 1)

            def normalise_x2(r, first=False):
                dve.wait_ge(rstd2_ready, r + 1)
                if not first:
                    dve.wait_ge(x2T_ready, r)
                for i in range(2):
                    step = nc.vector.tensor_scalar(xn2[:, i, :], rows[:, bass.ds(2 * r + i, 1), 0:D].rearrange("p o w -> p (o w)"),
                                                   mv2[:, i, 0:1], rstd2[:, i:i + 1], ALU.subtract, ALU.mult)
                step.then_inc(xn2_ready, 1)

            def copy_x2T(r, first=False):
                dve.wait_ge(x2T_ready, r + 1)
                if not first:
                    dve.wait_ge(logits_ready, r)
                nc.vector.tensor_copy(xn2T[:, :, :].rearrange("p i k -> p (i k)"), bank[:, MISC, 0:2 * P]).then_inc(xn2T_ready, 1)

            def choose(r, first=False):
                base = 4 * r
                dve.wait_ge(logits_ready, r + 1)
                if not first:
                    dve.wait_ge(lexp_ready, r)
                nc.vector.tensor_copy(logits[:, :, :].rearrange("p i e -> p (i e)"), bank[:, MISC, 0:2 * E]).then_inc(logits_copied, 1)
                dve.wait_ge(logits_copied, r + 1)
                nc.vector.tensor_reduce(neg_lmax[:, :], logits[:, :, :], AX, ALU.max, negate=True).then_inc(neg_lmax_ready, 1)
                dve.wait_ge(neg_lmax_ready, r + 1)
                nc.vector.tensor_tensor(is_max[:, :, :], logits[:, :, :],
                                        neg_lmax[:, :].unsqueeze(2).to_broadcast([P, 2, E]), ALU.add).then_inc(router_step, 1)
                dve.wait_ge(router_step, base + 1)
                nc.vector.scalar_tensor_tensor(is_max[:, :, :], is_max[:, :, :], 0.0,
                                               rev[:, :].unsqueeze(1).to_broadcast([P, 2, E]),
                                               ALU.is_equal, ALU.mult).then_inc(router_step, 1)
                dve.wait_ge(router_step, base + 2)
                nc.vector.tensor_reduce(first_max[:, :], is_max[:, :, :], AX, ALU.max).then_inc(router_step, 1)
                dve.wait_ge(router_step, base + 3)
                if not first:
                    dve.wait_ge(rank_ready, r)
                nc.vector.tensor_tensor(onehot[:, :, :], rev[:, :].unsqueeze(1).to_broadcast([P, 2, E]),
                                        first_max[:, :].unsqueeze(2).to_broadcast([P, 2, E]), ALU.is_equal).then_inc(router_step, 1)
                dve.wait_ge(router_step, base + 4)
                for i in range(2):
                    nc.vector.tensor_tensor(running[:, bass.ds(2 * r + i + 1, 1), :].rearrange("p o e -> p (o e)"),
                                            running[:, bass.ds(2 * r + i, 1), :].rearrange("p o e -> p (o e)"),
                                            onehot[:, i, :], ALU.add).then_inc(running_step, 1)
                    dve.wait_ge(running_step, 2 * r + i + 1)

            def put_place(r, first=False):
                base = 4 * r
                dve.wait_ge(rank_ready, r + 1)
                nc.vector.tensor_tensor(place[:, :, :], bank[:, MISC, 0:2 * E].rearrange("p (i e) -> p i e", i=2),
                                        region_no[:, :].unsqueeze(1).to_broadcast([P, 2, E]), ALU.add).then_inc(rank_read, 1)
                dve.wait_ge(lexp_ready, r + 1)
                nc.vector.reciprocal(lrec[:, :], lsum[:, :]).then_inc(place_step, 1)
                dve.wait_ge(rank_read, r + 1)
                nc.vector.tensor_tensor(place[:, :, :], place[:, :, :], onehot[:, :, :], ALU.mult).then_inc(place_step, 1)
                dve.wait_ge(place_step, base + 1)
                nc.vector.tensor_scalar(rows[:, bass.ds(2 * r, 2), GATE:GATE + 1], lrec[:, :].unsqueeze(2), tg[:, 1:2], None,
                                        ALU.mult).then_inc(place_step, 1)
                dve.wait_ge(place_step, base + 2)
                nc.vector.reduce_sum(place_f[:, :], place[:, :, :], AX).then_inc(place_step, 1)
                dve.wait_ge(place_step, base + 4)
                if not first:
                    for i in range(2):
                        dve.wait_ge(scattered[i], 16 * r)
                nc.vector.tensor_copy(place_i[:, :], place_f[:, :]).then_inc(place_ready, 1)

            def pair(j, first=False, last=False, norm=True, early=False):
                if not last:
                    copy_xT(j + 1)
                if norm:
                    normalise_x(j + 2)
                if not first:
                    if not early:
                        dve.wait_ge(mv2_used, j - 1)
                    residual(2 * j - 1, 1)
                    aggregate_x2(j - 1, j)
                invert_sums(2 * j + 1, 1, first)
                if not last:
                    head_max(2 * j + 2, 0)
                if not first:
                    normalise_x2(j - 1, early)
                residual(2 * j, 0)
                if not first:
                    copy_x2T(j - 1, early)
                if not last:
                    invert_sums(2 * j + 2, 0)
                if not first:
                    choose(j - 1, early)
                if not last:
                    head_max(2 * j + 3, 1)
                if not first:
                    put_place(j - 1, early)

            def empty_all(lo, hi):
                for n in range(lo, hi):
                    what, i, b, who = groups[n]
                    if who == "dve":
                        dve.wait_ge(setup_ready, n + 1)
                        if what == "vwT" and i == 0:
                            dve.wait_ge(tanh_ready, 1)
                        empty(nc.vector, n, b, what, i).then_inc(setup_dve, 1)

            normalise_x(0, True)
            empty_all(0, len(k_side))
            copy_xT(0, True)
            normalise_x(1)
            head_max(0, 0, True)
            head_max(1, 1, True)
            dve.wait_ge(bo_in, 16)
            dve.wait_ge(tanh_ready, 1)
            nc.vector.tensor_scalar(bo4[:, :, :], bo_row[:, :].unsqueeze(1).to_broadcast([1, B, D]), tg[0:1, 0:1], None,
                                    ALU.mult).then_inc(bo4_ready, 1)
            invert_sums(0, 0, True)
            empty_all(len(k_side), len(groups))
            dve.wait_ge(consts, CONSTS)
            pair(0, first=True)
            pair(1, early=True)
            with dve.Fori(2, NPAIR - 2) as j:
                pair(j)
            pair(NPAIR - 2, norm=False)
            pair(NPAIR - 1, last=True, norm=False)
            r = NPAIR - 1
            dve.wait_ge(mv2_used, r)
            residual(T - 1, 1)
            aggregate_x2(r, r + 1)
            normalise_x2(r)
            copy_x2T(r)
            choose(r)
            put_place(r)

            done = [0]

            def plan(step):
                step.then_inc(plan_step, 1)
                done[0] += 1
                dve.wait_ge(plan_step, done[0])

            def over_tiles(v):
                return v.unsqueeze(1).to_broadcast([P, NJ, E])

            by_tile = tile_no[:, :].unsqueeze(2).to_broadcast([P, NJ, E])
            dve.wait_ge(cnt_ready, 1)
            plan(nc.vector.tensor_copy(cnt[:, :], bank[:, MISC, 0:E]))
            plan(nc.vector.tensor_tensor(above[:, :, :], cnt[:, :].unsqueeze(2).to_broadcast([P, E, T]),
                                         tile_edge[:, :].unsqueeze(1).to_broadcast([P, E, T]), ALU.is_gt))
            plan(nc.vector.reduce_sum(ntiles[:, :], above[:, :, :], AX))
            plan(nc.vector.tensor_tensor_scan(cum_in[:, :], ones8[:, :], ntiles[:, :], 0.0, ALU.mult, ALU.add))
            plan(nc.vector.tensor_tensor(cum_ex[:, :], cum_in[:, :], ntiles[:, :], ALU.subtract))
            plan(nc.vector.tensor_tensor(sel[:, :, :], by_tile, over_tiles(cum_ex[:, :]), ALU.is_ge))
            plan(nc.vector.tensor_tensor(sel2[:, :, :], by_tile, over_tiles(cum_in[:, :]), ALU.is_lt))
            plan(nc.vector.tensor_tensor(sel[:, :, :], sel[:, :, :], sel2[:, :, :], ALU.mult))
            plan(nc.vector.tensor_tensor(picked[:, 0, :, :], sel[:, :, :], over_tiles(cum_ex[:, :]), ALU.mult))
            plan(nc.vector.tensor_tensor(picked[:, 1, :, :], sel[:, :, :], over_tiles(cnt[:, :]), ALU.mult))
            plan(nc.vector.tensor_tensor(picked[:, 2, :, :], sel[:, :, :], over_tiles(expert_no[:, :]), ALU.mult))
            plan(nc.vector.reduce_sum(pick[:, :, :], picked[:, :, :, :], AX))
            first_tile, count, expert = pick[:, 0, :], pick[:, 1, :], pick[:, 2, :]
            plan(nc.vector.tensor_tensor(wanted[:, :], tile_no[:, :], first_tile, ALU.subtract))
            plan(nc.vector.tensor_scalar(wanted[:, :], wanted[:, :], float(P), None, ALU.mult))
            plan(nc.vector.tensor_scalar(last_start[:, :], count, float(-P), 0.0, ALU.add, ALU.max))
            plan(nc.vector.tensor_tensor(start[:, :], wanted[:, :], last_start[:, :], ALU.min))
            plan(nc.vector.scalar_tensor_tensor(row_f[:, :], expert, float(REGION), start[:, :], ALU.mult, ALU.add))
            plan(nc.vector.tensor_copy(row_i[:, :], row_f[:, :]))
            plan(nc.vector.tensor_copy(expert_i[:, :], expert))
            plan(nc.vector.tensor_tensor(low[:, :], wanted[:, :], start[:, :], ALU.subtract))
            plan(nc.vector.tensor_tensor(high[:, :], count, start[:, :], ALU.subtract))
            plan(nc.vector.tensor_scalar(low[:, :], low[:, :], part_no[:, :], None, ALU.is_le))
            plan(nc.vector.tensor_scalar(high[:, :], high[:, :], part_no[:, :], None, ALU.is_gt))
            plan(nc.vector.tensor_tensor(drop[:, :], low[:, :], high[:, :], ALU.mult))
            plan(nc.vector.tensor_scalar(drop[:, :], drop[:, :], -DROP, DROP, ALU.mult, ALU.add))
            assert done[0] == PLAN_STEPS

            def erow(j, lo, hi):
                return erows[:, bass.ds(j, 1), lo:hi].rearrange("p o w -> p (o w)")

            def normalise_rows(j, s, k, uses, first=False):
                dve.wait_ge(erows_in[k], 16 * uses)
                if not first:
                    dve.wait_ge(exT_psum, j - 1)
                nc.vector.tensor_scalar(exn[:, s, :], erow(j, 0, D), erow(j, MEAN, MEAN + 1), erow(j, RSTD, RSTD + 1),
                                        ALU.subtract, ALU.mult).then_inc(exn_ready, 1)

            def copy_rowsT(j, s, first=False):
                dve.wait_ge(exT_psum, j + 1)
                if not first:
                    dve.wait_ge(h_ready, j - 1)
                nc.vector.tensor_copy(exT[:, s, :], bank[:, s, 0:P]).then_inc(exT_ready, 1)

            def add_b1(j, s, first=False):
                expert = dve.value_load(expert_i[0:1, bass.ds(j, 1)], min_val=0, max_val=E - 1)
                dve.wait_ge(h_ready, j + 1)
                if not first:
                    dve.wait_ge(hid_ready, j - 1)
                nc.vector.tensor_tensor(hbias[:, s, :, :], bank[:, 2 + s, :].rearrange("p (c k) -> p c k", c=FC),
                                        b1T[:, bass.ds(expert * FC, FC)].unsqueeze(2).to_broadcast([P, FC, P]),
                                        ALU.add).then_inc(hbias_ready, 1)

            def finish(j, s, k, uses, first=False):
                expert = dve.value_load(expert_i[0:1, bass.ds(j, 1)], min_val=0, max_val=E - 1)
                dve.wait_ge(y_ready, j + 1)
                nc.vector.tensor_tensor(ybias[:, s, :], bank[:, 4 + s, 0:D], b2_bc[:, bass.ds(expert * D, D)],
                                        ALU.add).then_inc(ybias_ready, 1)
                if not first:
                    dve.wait_ge(stored[k], 16 * (uses - 1))
                nc.vector.tensor_scalar(token_i[:, k:k + 1], erow(j, TOKEN, TOKEN + 1), drop[:, bass.ds(j, 1)], None,
                                        ALU.add).then_inc(token_ready[k], 1)
                dve.wait_ge(ybias_ready, j + 1)
                nc.vector.scalar_tensor_tensor(eout[:, k, :], ybias[:, s, :], erow(j, GATE, GATE + 1), erow(j, 0, D),
                                               ALU.mult, ALU.add).then_inc(eout_ready[k], 1)

            def slot(j, k, uses, first=False):
                whole = not isinstance(j, int)
                if whole or j + 3 < NJ:
                    normalise_rows(j + 3, (k + 3) % 2, (k + 3) % NW, uses + (k + 3) // NW)
                if whole or j + 2 < NJ:
                    copy_rowsT(j + 2, k % 2)
                if whole or j + 1 < NJ:
                    add_b1(j + 1, (k + 1) % 2, isinstance(j, int) and j < 1)
                finish(j, k % 2, k, uses, isinstance(j, int) and j < NW)

            dve.wait_ge(b2_in, 16)
            normalise_rows(0, 0, 0, 1, True)
            normalise_rows(1, 1, 1, 1, True)
            copy_rowsT(0, 0, True)
            copy_rowsT(1, 1, True)
            normalise_rows(2, 0, 2, 1)
            add_b1(0, 0, True)
            for j in range(NW):
                slot(j, j, 1)
            with dve.Fori(1, (NJ - 3) // NW) as q:
                for k in range(NW):
                    slot(NW * q + k, k, q + 1)
            for j in range((NJ - 3) // NW * NW, NJ):
                slot(j, j % NW, j // NW + 1)


PLAN_STEPS = 25
CONSTS = 14


_INS = ['x', 'ctx_768', 'g_xattn', 'g_ffn', 'L0_xattn_Wq', 'L0_xattn_Wk', 'L0_xattn_Wv', 'L0_xattn_Wo', 'L0_xattn_bo',
        'L0_ffn_Wr', 'L0_ffn_W1', 'L0_ffn_b1', 'L0_ffn_W2', 'L0_ffn_b2']
_OUTS = [((4, 512, 128), 'float32')]


def kernel(**inputs):
    import numpy as _np
    import concourse.bacc as _bacc
    from concourse import mybir as _mybir
    from concourse.bass_utils import run_bass_kernel_spmd as _run

    nc = _bacc.Bacc("TRN2", target_bir_lowering=False, num_devices=1)
    arrays, args = {}, []
    for name in _INS:
        a = _np.ascontiguousarray(inputs[name])
        arrays[f"in_{name}_dram"] = a
        args.append(nc.dram_tensor(f"in_{name}_dram", a.shape, _mybir.dt.from_np(a.dtype), kind="ExternalInput").ap())
    for i, (shape, dtype) in enumerate(_OUTS):
        dt = _mybir.dt.from_np(_np.dtype(dtype))
        args.append(nc.dram_tensor(f"out_{i}_dram", shape, dt, kind="ExternalOutput").ap())
    flamingo_block(nc, *args)
    r = _run(nc, [arrays], core_ids=[0])
    got = tuple(r.results[0][f"out_{i}_dram"] for i in range(len(_OUTS)))
    return got[0]
```

```python
from contextlib import ExitStack

import concourse.bass as bass
from concourse import mybir

F32 = mybir.dt.float32
BF16 = mybir.dt.bfloat16
I32 = mybir.dt.int32
ALU = mybir.AluOpType
ACT = mybir.ActivationFunctionType
AX = mybir.AxisListType.X

P = 128
EPS = 1e-5


def flamingo_block(nc, x, ctx_t, g_xattn, g_ffn, Wq_t, Wk, Wv, Wo, bo, Wr, W1b1, W2, b2, out):
    B, S, D = x.shape
    C, _, L = ctx_t.shape
    INNER = Wq_t.shape[0]
    DH = 64
    H = INNER // DH
    E, F, _ = W2.shape
    assert W1b1.shape == (E, P, F + F // P)
    T = B * S // P
    NPAIR = T // 2
    PAIRS_PER_BATCH = S // P // 2
    HC = INNER // P
    HPC = P // DH
    FC = F // P
    HL = H * L
    HALF = HL // 2
    NCH = -(-HL // P)
    LASTC = HL - (NCH - 1) * P
    BL = B * L
    SCALE = float(DH) ** -0.5
    NTOK = B * S
    REGION = NTOK
    NJ = T + E - 1
    ROW = D + 4
    MEAN, RSTD, GATE, TOKEN = D, D + 1, D + 2, D + 3
    NW = 4
    DROP = float(2 * NTOK)
    assert D == P and H % 2 == 0 and LASTC < P and 4 * P == 512

    x_rows = x.rearrange("b s d -> (b s) d")
    out_rows = out.rearrange("b s d -> (b s) d")
    x_tiles = x_rows.rearrange("(t p) d -> p t d", p=P)
    scratch = nc.dram_tensor("expert_rows", [E * REGION, ROW], F32, kind="Internal").ap()

    with ExitStack() as es:
        def sb(name, shape, dt=F32):
            return es.enter_context(nc.sbuf_tensor(name, shape, dt))

        def sem(name):
            return es.enter_context(nc.semaphore(name))

        ctxT = sb("ctxT", [C, BL])
        wqT = sb("wqT", [P, HC, P])
        wk_sb = sb("wk_sb", [C, INNER])
        wv_sb = sb("wv_sb", [C, INNER])
        wo_sb = sb("wo_sb", [P, HC, D])
        kT = sb("kT", [P, HC, BL])
        vT = sb("vT", [P, HC, BL])
        A = sb("A", [P, B * HL])
        vwT = sb("vwT", [P, B, HL])
        vw = sb("vw", [P, B, NCH, D])
        wr_sb = sb("wr_sb", [P, E])
        w2_sb = sb("w2_sb", [P, E * FC * D])
        b2_bc = sb("b2_bc", [P, E * D])
        gates = sb("gates", [P, 2])
        tg = sb("tg", [P, 2])
        bo_row = sb("bo_row", [1, D])
        bo4 = sb("bo4", [1, B, D])
        ident = sb("ident", [P, P])
        tri = sb("tri", [P, P], BF16)
        ones_bf = sb("ones_bf", [P, P], BF16)
        rev = sb("rev", [P, E])
        expert_no = sb("expert_no", [P, E])
        region_no = sb("region_no", [P, E])
        ones8 = sb("ones8", [P, E])
        tile_edge = sb("tile_edge", [P, T])
        tile_no = sb("tile_no", [P, NJ])
        part_no = sb("part_no", [P, 1])
        pad = sb("pad", [P, ROW])
        x_sb = sb("x_sb", [P, T, D])
        stats1 = sb("stats1", [P, T, 6])
        mv1 = sb("mv1", [P, T, 2])
        rstd1 = sb("rstd1", [P, T])
        xn = sb("xn", [P, 2, D])
        xnT = sb("xnT", [P, 2, P])
        negmax = sb("negmax", [P, 2, H])
        expsum = sb("expsum", [P, 2, H])
        rsum = sb("rsum", [P, 2, H])
        probs = sb("probs", [P, 2, HL + 1])
        probsT = sb("probsT", [P, 2, NCH, P])
        rows = sb("rows", [P, T, ROW])
        stats2 = sb("stats2", [P, 2, 6])
        mv2 = sb("mv2", [P, 2, 2])
        var2 = sb("var2", [P, 2])
        rstd2 = sb("rstd2", [P, 2])
        xn2 = sb("xn2", [P, 2, D])
        eps = sb("eps", [P, 2])
        minus_half = sb("minus_half", [P, T])
        xn2T = sb("xn2T", [P, 2, P])
        logits = sb("logits", [P, 2, E])
        neg_lmax = sb("neg_lmax", [P, 2])
        below_max = sb("below_max", [P, 2, E])
        is_max = sb("is_max", [P, 2, E])
        first_max = sb("first_max", [P, 2])
        onehot = sb("onehot", [P, 2, E], BF16)
        running = sb("running", [P, T + 1, E], BF16)
        lexp = sb("lexp", [P, 2, E])
        lsum = sb("lsum", [P, 2])
        lrec = sb("lrec", [P, 2])
        place = sb("place", [P, 2, E])
        place_f = sb("place_f", [P, 2])
        place_i = sb("place_i", [P, 2], I32)
        payload = sb("payload", [P, 2, ROW])
        cnt = sb("cnt", [P, E])
        above = sb("above", [P, E, T])
        ntiles = sb("ntiles", [P, E])
        cum_in = sb("cum_in", [P, E])
        cum_ex = sb("cum_ex", [P, E])
        sel = sb("sel", [P, NJ, E])
        sel2 = sb("sel2", [P, NJ, E])
        picked = sb("picked", [P, 3, NJ, E])
        pick = sb("pick", [P, 3, NJ])
        wanted = sb("wanted", [P, NJ])
        last_start = sb("last_start", [P, NJ])
        start = sb("start", [P, NJ])
        low = sb("low", [P, NJ])
        high = sb("high", [P, NJ])
        row_f = sb("row_f", [P, NJ])
        where_i = sb("where_i", [P, NJ, 2], I32)
        w2_at_i = sb("w2_at_i", [P, NJ], I32)
        b2_at_i = sb("b2_at_i", [P, NJ], I32)
        drop = sb("drop", [P, NJ])
        erows = sb("erows", [P, NJ, ROW])
        exn = sb("exn", [P, 2, D])
        exT = sb("exT", [P, 2, P])
        w1_sb = sb("w1_sb", [P, NW, F + FC])
        hbias = sb("hbias", [P, 2, FC, P])
        hid = sb("hid", [P, 2, FC, P])
        ybias = sb("ybias", [P, 2, D])
        eout = sb("eout", [P, NW, D])
        token_i = sb("token_i", [P, NW], I32)

        bank = es.enter_context(nc.psum_tensor("bank", [P, 8, 512], F32))
        PT0, PT1, ATT, MISC = 4, 5, 6, 7

        ctx_in, wq_in, wk_in, wv_in, wo_in = (sem(n) for n in ("ctx_in", "wq_in", "wk_in", "wv_in", "wo_in"))
        x_in = [sem(f"x_in{b}") for b in range(B)]
        gates_in, wr_in, bo_in, b2_in, w2_in = (sem(n) for n in ("gates_in", "wr_in", "bo_in", "b2_in", "w2_in"))
        pads_out, bias_row_in = sem("pads_out"), sem("bias_row_in")

        def sems(*names):
            return [sem(n) for n in names]

        def sem2(name):
            return [sem(f"{name}{s}") for s in range(2)]

        def semk(name):
            return [sem(f"{name}{k}") for k in range(NW)]

        memsets, consts, setup_ready, setup_act, setup_dve, tanh_ready, bo4_ready = sems(
            "memsets", "consts", "setup_ready", "setup_act", "setup_dve", "tanh_ready", "bo4_ready")
        stats1_ready, mv1_ready, var1_ready, rstd1_ready = sems("stats1_ready", "mv1_ready", "var1_ready", "rstd1_ready")
        xn_ready, xT_ready, xnT_ready = sems("xn_ready", "xT_ready", "xnT_ready")
        scores_ready, max_ready, exp_ready = sem2("scores_ready"), sem2("max_ready"), sem2("exp_ready")
        rsum_ready, probs_ready = sem2("rsum_ready"), sem2("probs_ready")
        pT_ready, probsT_ready = sem2("pT_ready"), sem2("probsT_ready")
        attn_ready, resid_ready, stats2_ready = sem2("attn_ready"), sem2("resid_ready"), sem2("stats2_ready")
        mv2_ready, var2_ready, rstd2_ready, stats_in_rows, xn2_ready, x2T_ready, xn2T_ready = sems(
            "mv2_ready", "var2_ready", "rstd2_ready", "stats_in_rows", "xn2_ready", "x2T_ready", "xn2T_ready")
        logits_ready, logits_copied, neg_lmax_ready, below_ready, marks_ready, first_ready, onehot_ready = sems(
            "logits_ready", "logits_copied", "neg_lmax_ready", "below_ready", "marks_ready", "first_ready", "onehot_ready")
        running_ready, lexp_ready = sem2("running_ready"), sem("lexp_ready")
        lsum_ready, lrec_ready, gate_ready, payload_ready = sems("lsum_ready", "lrec_ready", "gate_ready", "payload_ready")
        rank_ready, rank_read, own_ready, sum_ready, place_ready = sems(
            "rank_ready", "rank_read", "own_ready", "sum_ready", "place_ready")
        scattered = sem2("scattered")
        cnt_ready, plan_step = sem("cnt_ready"), sem("plan_step")
        erows_in, w1_in = semk("erows_in"), semk("w1_in")
        exn_ready, exT_psum, exT_ready = semk("exn_ready"), semk("exT_psum"), semk("exT_ready")
        h_ready, hbias_ready, hid_ready = semk("h_ready"), semk("hbias_ready"), semk("hid_ready")
        y_ready, ybias_ready, token_ready, eout_ready, stored = (
            semk("y_ready"), semk("ybias_ready"), semk("token_ready"), semk("eout_ready"), semk("stored"))

        k_side = [("kT", c, c, ("dve", "act")[c % 2]) for c in range(HC)]
        k_side += [("A", h, (4 + h) % 8, ("dve", "act")[h % 2]) for h in range(H)]
        v_side = [("vT", c, 4 + c, "dve") for c in range(HC)]
        v_side += [("vwT", h, 4 + h % 4, "dve") for h in range(H)]
        v_side += [("vw", b, 4 + b, "dve") for b in range(B)]
        v_side += [("vw_last", 0, 4, "dve")]
        groups = k_side + v_side

        def emptied(eng, n):
            who = groups[n][3]
            count = sum(1 for g in groups[:n + 1] if g[3] == who)
            eng.wait_ge(setup_act if who == "act" else setup_dve, count)

        def group(what, index):
            return next(n for n, g in enumerate(groups) if g[:2] == (what, index))

        def last_in_bank(b, before):
            return max((n for n, g in enumerate(groups[:before]) if g[2] == b), default=None)

        def empty(eng, src_bank, what, i):
            act = eng is nc.scalar

            def copy(dst, src, scale=None):
                if act:
                    return nc.scalar.activation(dst, src, ACT.Copy, scale=1.0 if scale is None else scale)
                if scale is None:
                    return nc.vector.tensor_copy(dst, src)
                return nc.vector.tensor_scalar(dst, src, scale, None, ALU.mult)

            per_b = bank[:, src_bank, 0:BL].rearrange("p (b l) -> p b l", b=B)
            if what == "kT":
                return copy(kT[:, i, :], bank[:, src_bank, 0:BL], SCALE)
            if what == "A":
                return copy(A[:, :].rearrange("p (b h l) -> p b h l", b=B, h=H)[:, :, i, :], per_b)
            if what == "vT":
                return copy(vT[:, i, :], bank[:, src_bank, 0:BL])
            if what == "vwT":
                return copy(vwT[:, :, i * L:(i + 1) * L], per_b, tg[:, 0:1])
            if what == "vw":
                return copy(vw[:, i, 0:NCH - 1, :].rearrange("p c d -> p (c d)"), bank[:, src_bank, :])
            return copy(vw[0:LASTC, :, NCH - 1, :], bank[0:LASTC, src_bank, :].rearrange("p (b d) -> p b d", b=B))

        def fixed_wait(eng):
            eng.wait_ge(consts, 1)

        def one(t, lo=0, hi=D):
            return lambda tensor: tensor[:, bass.ds(t, 1), lo:hi].rearrange("p o d -> p (o d)")

        LOOP = (3, NPAIR - 2)

        def pairs(eng, pair):
            for j in range(LOOP[0]):
                pair(j)
            with eng.Fori(*LOOP) as j:
                pair(j)
            pair(NPAIR - 2)
            pair(NPAIR - 1)

        def runs(j, lag=0, ahead=0):
            return not isinstance(j, int) or (j >= lag and j + ahead < NPAIR)

        def normalise_x(dve, p, first=False):
            if not first:
                dve.wait_ge(xT_ready, p)
            for i in range(2):
                step = nc.vector.tensor_scalar(xn[:, i, :], one(2 * p + i)(x_sb), one(2 * p + i, 0, 1)(mv1),
                                               rstd1[:, bass.ds(2 * p + i, 1)], ALU.subtract, ALU.mult)
            step.then_inc(xn_ready, 1)

        def copy_xT(dve, p):
            dve.wait_ge(xT_ready, p + 1)
            nc.vector.tensor_copy(xnT[:, :, :].rearrange("p i k -> p (i k)"), bank[:, MISC, 0:2 * P]).then_inc(xnT_ready, 1)

        def head_max(dve, p, s):
            dve.wait_ge(scores_ready[s], p + 1)
            nc.vector.tensor_reduce(negmax[:, s, :].rearrange("p (b h) -> p b h", b=2),
                                    bank[:, 2 * s:2 * s + 2, 0:HALF].rearrange("p b (h l) -> p b h l", l=L),
                                    AX, ALU.max, negate=True).then_inc(max_ready[s], 1)

        def invert_sums(dve, p, s):
            dve.wait_ge(exp_ready[s], p + 1)
            nc.vector.reciprocal(rsum[:, s, :], expsum[:, s, :]).then_inc(rsum_ready[s], 1)

        def residual(dve, p, s):
            dve.wait_ge(attn_ready[s], p + 1)
            x2 = one(2 * p + s)(rows)
            nc.vector.tensor_tensor(x2, bank[:, ATT, 0:D], one(2 * p + s)(x_sb), ALU.add).then_inc(resid_ready[s], 1)
            fixed_wait(dve)
            dve.wait_ge(resid_ready[s], p + 1)
            nc.vector.bn_stats(stats2[:, s, :], x2).then_inc(stats2_ready[s], 1)

        def aggregate_x2(dve, r):
            for i in range(2):
                fixed_wait(dve)
                dve.wait_ge(stats2_ready[i], r + 1)
                step = nc.vector.bn_aggr(mv2[:, i, :], stats2[:, i, :])
            step.then_inc(mv2_ready, 1)

        def normalise_x2(dve, r):
            dve.wait_ge(rstd2_ready, r + 1)
            for i in range(2):
                step = nc.vector.tensor_scalar(xn2[:, i, :], one(2 * r + i)(rows), mv2[:, i, 0:1], mv2[:, i, 1:2],
                                               ALU.subtract, ALU.mult)
            step.then_inc(xn2_ready, 1)
            nc.vector.tensor_copy(rows[:, bass.ds(2 * r, 2), MEAN:RSTD + 1], mv2[:, :, :]).then_inc(stats_in_rows, 1)

        def copy_x2T(dve, r):
            dve.wait_ge(x2T_ready, r + 1)
            nc.vector.tensor_copy(xn2T[:, :, :].rearrange("p i k -> p (i k)"), bank[:, MISC, 0:2 * P]).then_inc(xn2T_ready, 1)

        def by_expert(v):
            return v.unsqueeze(1).to_broadcast([P, 2, E])

        def by_token(v):
            return v.unsqueeze(2).to_broadcast([P, 2, E])

        def copy_logits(dve, r):
            dve.wait_ge(logits_ready, r + 1)
            nc.vector.tensor_copy(logits[:, :, :].rearrange("p i e -> p (i e)"), bank[:, MISC, 0:2 * E]).then_inc(logits_copied, 1)

        def max_logit(dve, r):
            dve.wait_ge(logits_copied, r + 1)
            nc.vector.tensor_reduce(neg_lmax[:, :], logits[:, :, :], AX, ALU.max, negate=True).then_inc(neg_lmax_ready, 1)

        def subtract_max(dve, r):
            dve.wait_ge(neg_lmax_ready, r + 1)
            if not (isinstance(r, int) and r < 1):
                dve.wait_ge(lexp_ready, r)
            nc.vector.tensor_tensor(below_max[:, :, :], logits[:, :, :], by_token(neg_lmax[:, :]), ALU.add).then_inc(below_ready, 1)

        def mark_maxima(dve, r):
            dve.wait_ge(below_ready, r + 1)
            nc.vector.scalar_tensor_tensor(is_max[:, :, :], below_max[:, :, :], 0.0, by_expert(rev[:, :]),
                                           ALU.is_equal, ALU.mult).then_inc(marks_ready, 1)

        def first_maximum(dve, r):
            dve.wait_ge(marks_ready, r + 1)
            nc.vector.tensor_reduce(first_max[:, :], is_max[:, :, :], AX, ALU.max).then_inc(first_ready, 1)

        def mark_expert(dve, r):
            dve.wait_ge(first_ready, r + 1)
            nc.vector.tensor_tensor(onehot[:, :, :], by_expert(rev[:, :]), by_token(first_max[:, :]), ALU.is_equal)\
                .then_inc(onehot_ready, 1)

        def count_tokens(dve, r, i):
            dve.wait_ge(running_ready[0], r + 1) if i else dve.wait_ge(onehot_ready, r + 1)
            nc.vector.tensor_tensor(one(2 * r + i + 1, 0, E)(running), one(2 * r + i, 0, E)(running),
                                    onehot[:, i, :], ALU.add).then_inc(running_ready[i], 1)

        def place_row(dve, r):
            dve.wait_ge(rank_ready, r + 1)
            nc.vector.tensor_tensor(place[:, :, :], bank[:, MISC, 0:2 * E].rearrange("p (i e) -> p i e", i=2),
                                    by_expert(region_no[:, :]), ALU.add).then_inc(rank_read, 1)
            dve.wait_ge(lexp_ready, r + 1)
            nc.vector.reduce_sum(lsum[:, :], lexp[:, :, :], AX).then_inc(lsum_ready, 1)
            dve.wait_ge(rank_read, r + 1)
            nc.vector.tensor_tensor(place[:, :, :], place[:, :, :], onehot[:, :, :], ALU.mult).then_inc(own_ready, 1)
            dve.wait_ge(lsum_ready, r + 1)
            nc.vector.reciprocal(lrec[:, :], lsum[:, :]).then_inc(lrec_ready, 1)
            dve.wait_ge(own_ready, r + 1)
            nc.vector.reduce_sum(place_f[:, :], place[:, :, :], AX).then_inc(sum_ready, 1)
            dve.wait_ge(lrec_ready, r + 1)
            nc.vector.tensor_scalar(rows[:, bass.ds(2 * r, 2), GATE:GATE + 1], lrec[:, :].unsqueeze(2), tg[:, 1:2], None,
                                    ALU.mult).then_inc(gate_ready, 1)

        def send_payload(dve, r):
            if not (isinstance(r, int) and r < 1):
                for i in range(2):
                    dve.wait_ge(scattered[i], 16 * r)
            dve.wait_ge(sum_ready, r + 1)
            nc.vector.tensor_copy(place_i[:, :], place_f[:, :]).then_inc(place_ready, 1)
            dve.wait_ge(gate_ready, r + 1)
            dve.wait_ge(stats_in_rows, r + 1)
            nc.vector.tensor_copy(payload[:, :, :], rows[:, bass.ds(2 * r, 2), :]).then_inc(payload_ready, 1)

        def slots(eng, slot):
            for j in range(NW + 1):
                slot(j, j % NW, j // NW)
            with eng.Fori(1, (NJ - 4) // NW) as q:
                for k in range(1, NW + 1):
                    slot(NW * q + k, k % NW, q + k // NW)
            for j in range((NJ - 4) // NW * NW + 1, NJ):
                slot(j, j % NW, j // NW)

        block = es.enter_context(nc.Block())

        @block.sync
        def _(sp):
            per = S // P
            sp.dma_start(ctxT[:, :], ctx_t.rearrange("c b l -> c (b l)")).then_inc(ctx_in, 16)
            sp.dma_start(wk_sb[:, :], Wk).then_inc(wk_in, 16)
            sp.dma_start(x_sb[:, 0:per, :], x_tiles[:, 0:per, :]).then_inc(x_in[0], 16)
            sp.dma_start(wv_sb[:, :], Wv).then_inc(wv_in, 16)
            sp.dma_start(wo_sb[:, :, :], Wo.rearrange("(c p) d -> p c d", p=P)).then_inc(wo_in, 16)
            for b in range(1, B):
                sp.dma_start(x_sb[:, b * per:(b + 1) * per, :], x_tiles[:, b * per:(b + 1) * per, :]).then_inc(x_in[b], 16)
            sp.wait_ge(memsets, 4)
            for e in range(E):
                sp.dma_start(scratch[e * REGION:e * REGION + P, :], pad[:, :]).then_inc(pads_out, 16)
            sp.wait_ge(bo4_ready, 1)
            sp.dma_start(vw[LASTC:LASTC + 1, :, NCH - 1, :], bo4[:, :, :]).then_inc(bias_row_in, 16)
            sp.dma_start(b2_bc[:, :], b2.rearrange("(o e) d -> o (e d)", o=1).partition_broadcast(P)).then_inc(b2_in, 16)
            sp.dma_start(w2_sb[:, :].rearrange("p (e c d) -> p e c d", e=E, c=FC),
                         W2.rearrange("e (c p) d -> p e c d", p=P)).then_inc(w2_in, 16)

            def load_tile(j, k):
                _, (row, w1_row) = nc.values_load_multi_w_load_instructions(
                    where_i[0:1, bass.ds(j, 1), :].rearrange("p o w -> p (o w)"), engines=[sp.engine],
                    min_val=0, max_val=E * REGION - P,
                    skip_runtime_bounds_check_because="the plan keeps every tile inside its expert's region")
                w1_row = nc.s_assert_within(w1_row, 0, (E - 1) * P, skip_runtime_bounds_check_because="an expert number times 128")
                sp.dma_start(erows[:, bass.ds(j, 1), :].rearrange("p o w -> p (o w)"),
                             scratch[bass.ds(row, P), :]).then_inc(erows_in[k], 16)
                sp.dma_start(w1_sb[:, k, :], W1b1.rearrange("e p f -> (e p) f")[bass.ds(w1_row, P), :])\
                    .then_inc(w1_in[k], 16)

            sp.wait_ge(plan_step, PLAN_STEPS)
            for s in range(2):
                sp.wait_ge(scattered[s], 16 * NPAIR)
            for j in range(NW):
                load_tile(j, j)
            with sp.Fori(1, NJ // NW) as q:
                for k in range(NW):
                    sp.wait_ge(hbias_ready[k], q)
                    load_tile(NW * q + k, k)
            for j in range(NJ // NW * NW, NJ):
                sp.wait_ge(hbias_ready[j % NW], j // NW)
                load_tile(j, j % NW)

        @block.gpsimd
        def _(pool):
            nc.gpsimd.memset(ident[:, :], 0.0).then_inc(memsets, 1)
            nc.gpsimd.memset(tri[:, :], 1.0).then_inc(memsets, 1)
            nc.gpsimd.memset(ones_bf[:, :], 1.0).then_inc(memsets, 1)
            nc.gpsimd.memset(pad[:, :], 0.0).then_inc(memsets, 1)
            nc.gpsimd.memset(minus_half[:, :], -0.5).then_inc(consts, 1)
            nc.gpsimd.memset(eps[:, :], EPS).then_inc(consts, 1)
            pool.wait_ge(memsets, 2)
            nc.gpsimd.affine_select(out=ident[:, :], in_=ident[:, :], compare_op=ALU.not_equal, fill=1.0,
                                    base=0, pattern=[[-1, P]], channel_multiplier=1).then_inc(consts, 1)
            nc.gpsimd.affine_select(out=tri[:, :], in_=tri[:, :], compare_op=ALU.is_gt, fill=0.0,
                                    base=0, pattern=[[1, P]], channel_multiplier=-1).then_inc(consts, 1)

            def count_up(dst, step, n, base=0, per_partition=0):
                nc.gpsimd.iota(dst, [[step, n]], base=base, channel_multiplier=per_partition,
                               allow_small_or_imprecise_dtypes=True).then_inc(consts, 1)

            count_up(rev[:, :], -1, E, base=E)
            count_up(expert_no[:, :], 1, E)
            count_up(region_no[:, :], REGION, E)
            count_up(tile_edge[:, :], P, T)
            count_up(tile_no[:, :], 1, NJ)
            count_up(part_no[:, :], 0, 1, per_partition=1)
            count_up(rows[:, :, TOKEN:TOKEN + 1].rearrange("p t o -> p (t o)"), P, T, per_partition=1)
            nc.gpsimd.memset(ones8[:, :], 1.0).then_inc(consts, 1)
            nc.gpsimd.memset(running[:, 0, :], 0.0).then_inc(consts, 1)
            nc.gpsimd.memset(probs[:, :, HL:HL + 1], 1.0).then_inc(consts, 1)
            pool.wait_ge(consts, CONSTS)
            for n, (lo, hi) in enumerate(((0, S // P), (S // P, T))):
                pool.wait_ge(var1_ready, n + 1)
                nc.gpsimd.tensor_tensor(rstd1[:, lo:hi], rstd1[:, lo:hi], minus_half[:, lo:hi], ALU.pow).then_inc(rstd1_ready, 1)

            def normalise(p, s):
                pool.wait_ge(rsum_ready[s], p + 1)
                v = probs[:, s, 0:HL].rearrange("p (h l) -> p h l", h=H)
                nc.gpsimd.tensor_tensor(v, v, rsum[:, s, :].unsqueeze(2).to_broadcast([P, H, L]), ALU.mult)\
                    .then_inc(probs_ready[s], 1)

            def invert_std(r):
                pool.wait_ge(mv2_ready, r + 1)
                nc.gpsimd.tensor_tensor(var2[:, :].unsqueeze(2), mv2[:, :, 1:2], eps[:, :].unsqueeze(2), ALU.add)\
                    .then_inc(var2_ready, 1)
                pool.wait_ge(var2_ready, r + 1)
                nc.gpsimd.tensor_tensor(mv2[:, :, 1:2], var2[:, :].unsqueeze(2), minus_half[:, 0:2].unsqueeze(2), ALU.pow)\
                    .then_inc(rstd2_ready, 1)

            def scatter(pairs_placed):
                fixed_wait(pool)
                pool.wait_ge(place_ready, pairs_placed)
                pool.wait_ge(payload_ready, pairs_placed)
                for i in range(2):
                    nc.gpsimd.indirect_dma_start(scratch, bass.IndirectOffsetOnAxis(place_i[:, i:i + 1], 0),
                                                 payload[:, i, :], None,
                                                 bounds_check=E * REGION - 1, oob_is_err=False)\
                        .then_inc(scattered[i], 16)

            def pair(j, placed):
                normalise(j, 1)
                if runs(j, lag=1):
                    invert_std(j - 1)
                if runs(j, lag=2):
                    scatter(placed)
                if runs(j, ahead=1):
                    normalise(j + 1, 0)

            normalise(0, 0)
            pool.wait_ge(pads_out, 16 * E)
            for j in range(LOOP[0]):
                pair(j, j - 1)
            with pool.Fori(LOOP[0] - 1, LOOP[1] - 1) as placed:
                pair(placed + 1, placed)
            pair(NPAIR - 2, NPAIR - 3)
            pair(NPAIR - 1, NPAIR - 2)
            invert_std(NPAIR - 1)
            scatter(NPAIR - 1)
            scatter(NPAIR)

            def store(k, uses):
                fixed_wait(pool)
                pool.wait_ge(eout_ready[k], uses)
                pool.wait_ge(token_ready[k], uses)
                nc.gpsimd.indirect_dma_start(out_rows, bass.IndirectOffsetOnAxis(token_i[:, k:k + 1], 0),
                                             eout[:, k, :], None, bounds_check=NTOK - 1, oob_is_err=False)\
                    .then_inc(stored[k], 16)

            with pool.Fori(1, NJ // NW + 1) as uses:
                for k in range(NW):
                    store(k, uses)
            for k in range(NJ % NW):
                store(k, NJ // NW + 1)
            for k in range(NW):
                pool.wait_ge(stored[k], 16 * len(range(k, NJ, NW)))

        @block.scalar
        def _(act):
            act.dma_start(wqT[:, :, :], Wq_t.rearrange("(c p) d -> p c d", p=P)).then_inc(wq_in, 16)
            act.dma_start(gates[:, 0:1], g_xattn.rearrange("(o g) -> o g", o=1).partition_broadcast(P)).then_inc(gates_in, 16)
            act.dma_start(gates[:, 1:2], g_ffn.rearrange("(o g) -> o g", o=1).partition_broadcast(P)).then_inc(gates_in, 16)
            act.dma_start(bo_row[:, :], bo.rearrange("(o d) -> o d", o=1)).then_inc(bo_in, 16)
            act.dma_start(wr_sb[:, :], Wr).then_inc(wr_in, 16)
            act.wait_ge(gates_in, 32)
            nc.scalar.activation(tg[:, :], gates[:, :], ACT.Tanh).then_inc(tanh_ready, 1)
            for n, (what, i, b, who) in enumerate(groups):
                if who == "act":
                    act.wait_ge(setup_ready, n + 1)
                    empty(nc.scalar, b, what, i).then_inc(setup_act, 1)

            def exps(p, s):
                act.wait_ge(max_ready[s], p + 1)
                if not (isinstance(p, int) and p < 1):
                    act.wait_ge(pT_ready[s], p)
                for h in range(H):
                    src = bank[:, 2 * s + h // (H // 2), (h % (H // 2)) * L:(h % (H // 2) + 1) * L]
                    step = nc.scalar.activation(probs[:, s, h * L:(h + 1) * L], src, ACT.Exp,
                                                bias=negmax[:, s, h:h + 1], accum_out=expsum[:, s, h:h + 1])
                step.then_inc(exp_ready[s], 1)

            def copy_probsT(p, s):
                act.wait_ge(pT_ready[s], p + 1)
                nc.scalar.activation(probsT[:, s, 0:NCH - 1, :].rearrange("p c k -> p (c k)"),
                                     bank[:, PT0, :], ACT.Copy)
                nc.scalar.activation(probsT[0:LASTC + 1, s, NCH - 1, :], bank[0:LASTC + 1, PT1, 0:P], ACT.Copy)\
                    .then_inc(probsT_ready[s], 1)

            def router_exps(r):
                act.wait_ge(below_ready, r + 1)
                if not (isinstance(r, int) and r < 1):
                    act.wait_ge(lsum_ready, r)
                nc.scalar.activation(lexp[:, :, :].rearrange("p i e -> p (i e)"),
                                     below_max[:, :, :].rearrange("p i e -> p (i e)"), ACT.Exp).then_inc(lexp_ready, 1)

            def pair(j):
                exps(j, 1)
                copy_probsT(j, 0)
                if runs(j, lag=2):
                    router_exps(j - 2)
                if runs(j, ahead=1):
                    exps(j + 1, 0)
                copy_probsT(j, 1)

            exps(0, 0)
            pairs(act, pair)
            router_exps(NPAIR - 2)
            router_exps(NPAIR - 1)

            def copy_rowsT(k, uses):
                act.wait_ge(exT_psum[k], uses)
                if k < 2 and isinstance(uses, int) and uses < 2:
                    pass
                else:
                    act.wait_ge(h_ready[(k - 2) % NW], uses - (k < 2))
                nc.scalar.activation(exT[:, k % 2, :], bank[:, k % 2, 0:P], ACT.Copy).then_inc(exT_ready[k], 1)

            def gelu(k, uses):
                act.wait_ge(hbias_ready[k], uses)
                if not (k < 2 and isinstance(uses, int) and uses < 2):
                    act.wait_ge(y_ready[(k - 2) % NW], uses - (k < 2))
                nc.scalar.activation(hid[:, k % 2, :, :].rearrange("p c k -> p (c k)"),
                                     hbias[:, k % 2, :, :].rearrange("p c k -> p (c k)"), ACT.Gelu)\
                    .then_inc(hid_ready[k], 1)

            def slot(j, k, q):
                if not isinstance(j, int) or j + 2 < NJ:
                    copy_rowsT((k + 2) % NW, q + 1 + (k + 2) // NW)
                if not isinstance(j, int) or j + 1 < NJ:
                    gelu((k + 1) % NW, q + 1 + (k + 1) // NW)

            copy_rowsT(0, 1)
            copy_rowsT(1, 1)
            gelu(0, 1)
            slots(act, slot)

        @block.tensor
        def _(pe):
            def setup(lo, hi):
                for n in range(lo, hi):
                    what, i, b, _ = groups[n]
                    if (prev := last_in_bank(b, n)) is not None:
                        emptied(pe, prev)
                    if what in ("kT", "vT"):
                        pe.wait_ge(wk_in if what == "kT" else wv_in, 16)
                        pe.wait_ge(ctx_in, 16)
                        w = wk_sb if what == "kT" else wv_sb
                        step = nc.tensor.matmul(bank[:, b, 0:BL], w[:, i * P:(i + 1) * P], ctxT[:, :], start=True, stop=True)
                    elif what in ("A", "vwT"):
                        c, at = i // HPC, (i % HPC) * DH
                        emptied(pe, group("kT" if what == "A" else "vT", c))
                        pe.wait_ge(wq_in if what == "A" else wo_in, 16)
                        w, m = (wqT, kT) if what == "A" else (wo_sb, vT)
                        step = nc.tensor.matmul(bank[:, b, 0:BL], w[at:at + DH, c, :], m[at:at + DH, c, :], start=True, stop=True)
                    elif what == "vw":
                        emptied(pe, group("vwT", H - 1))
                        for c in range(NCH - 1):
                            step = nc.tensor.transpose(bank[:, b, c * P:(c + 1) * P], vwT[:, i, c * P:(c + 1) * P], ident[:, :])
                    else:
                        for k in range(B):
                            step = nc.tensor.transpose(bank[0:LASTC, b, k * P:(k + 1) * P], vwT[:, k, (NCH - 1) * P:HL], ident[:, :])
                    step.then_inc(setup_ready, 1)

            def transpose_x(p, guard=None):
                pe.wait_ge(xn_ready, p + 1)
                if guard is not None:
                    pe.wait_ge(*guard)
                for i in range(2):
                    step = nc.tensor.transpose(bank[:, MISC, i * P:(i + 1) * P], xn[:, i, :], ident[:, :])
                step.then_inc(xT_ready, 1)

            def scores(p, s):
                pe.wait_ge(xnT_ready, p + 1)
                if not (isinstance(p, int) and p < 1):
                    pe.wait_ge(exp_ready[s], p)
                for half in range(2):
                    step = nc.tensor.matmul(bank[:, 2 * s + half, 0:HALF], xnT[:, s, :],
                                            A[:, bass.ds(p // PAIRS_PER_BATCH * HL + half * HALF, HALF)],
                                            start=True, stop=True)
                step.then_inc(scores_ready[s], 1)

            def transpose_probs(p, s):
                pe.wait_ge(probs_ready[s], p + 1)
                if isinstance(p, int) and p < 1 and s == 0:
                    emptied(pe, last_in_bank(PT0, len(groups)))
                    emptied(pe, last_in_bank(PT1, len(groups)))
                else:
                    pe.wait_ge(probsT_ready[1 - s], p + s)
                for c in range(NCH - 1):
                    nc.tensor.transpose(bank[:, PT0, c * P:(c + 1) * P], probs[:, s, c * P:(c + 1) * P], ident[:, :])
                nc.tensor.transpose(bank[0:LASTC + 1, PT1, 0:P], probs[:, s, (NCH - 1) * P:HL + 1], ident[:, :])\
                    .then_inc(pT_ready[s], 1)

            def attend(p, s):
                pe.wait_ge(probsT_ready[s], p + 1)
                if isinstance(p, int) and p < 1 and s == 0:
                    pe.wait_ge(bias_row_in, 16)
                    emptied(pe, last_in_bank(ATT, len(groups)))
                    emptied(pe, len(groups) - 1)
                else:
                    pe.wait_ge(resid_ready[1 - s], p + s)
                for c in range(NCH):
                    k = P if c < NCH - 1 else LASTC + 1
                    step = nc.tensor.matmul(bank[:, ATT, 0:D], probsT[0:k, s, c, :],
                                            vw[0:k, bass.ds(p // PAIRS_PER_BATCH, 1), c, :].rearrange("p o d -> p (o d)"),
                                            start=c == 0, stop=c == NCH - 1)
                step.then_inc(attn_ready[s], 1)

            def transpose_x2(r, guard):
                pe.wait_ge(xn2_ready, r + 1)
                pe.wait_ge(*guard)
                for i in range(2):
                    step = nc.tensor.transpose(bank[:, MISC, i * P:(i + 1) * P], xn2[:, i, :], ident[:, :])
                step.then_inc(x2T_ready, 1)

            def router(r):
                pe.wait_ge(xn2T_ready, r + 1)
                pe.wait_ge(wr_in, 16)
                for i in range(2):
                    step = nc.tensor.matmul(bank[:, MISC, i * E:(i + 1) * E], xn2T[:, i, :], wr_sb[:, :], start=True, stop=True)
                step.then_inc(logits_ready, 1)

            def ranks(r):
                pe.wait_ge(onehot_ready, r + 1)
                pe.wait_ge(running_ready[0], r + 1)
                nc.tensor.matmul(bank[:, MISC, 0:2 * E], tri[:, :], onehot[:, :, :].rearrange("p i e -> p (i e)"),
                                 start=True, stop=False)
                nc.tensor.matmul(bank[:, MISC, 0:2 * E], ones_bf[:, :],
                                 running[:, bass.ds(2 * r, 2), :].rearrange("p i e -> p (i e)"),
                                 start=False, stop=True).then_inc(rank_ready, 1)

            def pair(j):
                if runs(j, ahead=1):
                    scores(j + 1, 0)
                transpose_probs(j, 0)
                if runs(j, lag=2):
                    ranks(j - 2)
                if runs(j, lag=1):
                    attend(j - 1, 1)
                if runs(j, ahead=1):
                    scores(j + 1, 1)
                if runs(j, ahead=2):
                    transpose_x(j + 2, (rank_read, j - 1) if runs(j, lag=2) else (xnT_ready, j + 2))
                transpose_probs(j, 1)
                if runs(j, lag=1):
                    transpose_x2(j - 1, (xnT_ready, j + 3) if runs(j, ahead=2) else (rank_read, j - 1))
                attend(j, 0)
                if runs(j, lag=1):
                    router(j - 1)

            pe.wait_ge(consts, CONSTS)
            setup(0, len(k_side))
            transpose_x(0, (setup_dve if groups[last_in_bank(MISC, len(k_side))][3] == "dve" else setup_act,
                            sum(1 for g in groups[:last_in_bank(MISC, len(k_side)) + 1]
                                if g[3] == groups[last_in_bank(MISC, len(k_side))][3])))
            for b in range(4):
                emptied(pe, last_in_bank(b, len(k_side)))
            emptied(pe, group("A", H - 1))
            emptied(pe, group("A", H - 2))
            scores(0, 0)
            scores(0, 1)
            transpose_x(1, (xnT_ready, 1))
            pe.wait_ge(xnT_ready, 2)
            setup(len(k_side), len(groups))
            emptied(pe, last_in_bank(MISC, len(groups)))
            pairs(pe, pair)
            r = NPAIR - 1
            ranks(r - 1)
            attend(r, 1)
            transpose_x2(r, (rank_read, r))
            router(r)
            ranks(r)
            pe.wait_ge(rank_read, NPAIR)
            pe.wait_ge(running_ready[1], NPAIR)
            nc.tensor.matmul(bank[:, MISC, 0:E], ones_bf[:, :], running[:, T, :], start=True, stop=True).then_inc(cnt_ready, 1)

            def transpose_rows(k, uses):
                pe.wait_ge(exn_ready[k], uses)
                if not (k < 2 and isinstance(uses, int) and uses < 2):
                    pe.wait_ge(exT_ready[(k - 2) % NW], uses - (k < 2))
                nc.tensor.transpose(bank[:, k % 2, 0:P], exn[:, k % 2, :], ident[:, :]).then_inc(exT_psum[k], 1)

            def hidden(k, uses):
                pe.wait_ge(exT_ready[k], uses)
                pe.wait_ge(w1_in[k], 16 * uses)
                if not (k < 2 and isinstance(uses, int) and uses < 2):
                    pe.wait_ge(hbias_ready[(k - 2) % NW], uses - (k < 2))
                for c in range(FC):
                    step = nc.tensor.matmul(bank[:, 2 + k % 2, c * P:(c + 1) * P], w1_sb[:, k, c * P:(c + 1) * P],
                                            exT[:, k % 2, :], start=True, stop=True)
                step.then_inc(h_ready[k], 1)

            def outputs(j, k, uses):
                w2_at = pe.value_load(w2_at_i[0:1, bass.ds(j, 1)], min_val=0, max_val=(E - 1) * FC * D)
                pe.wait_ge(hid_ready[k], uses)
                if not (k < 2 and isinstance(uses, int) and uses < 2):
                    pe.wait_ge(ybias_ready[(k - 2) % NW], uses - (k < 2))
                for c in range(FC):
                    step = nc.tensor.matmul(bank[:, 4 + k % 2, 0:D], hid[:, k % 2, c, :],
                                            w2_sb[:, bass.ds(w2_at + c * D, D)], start=c == 0, stop=c == FC - 1)
                step.then_inc(y_ready[k], 1)

            pe.wait_ge(w2_in, 16)
            pe.wait_ge(plan_step, PLAN_STEPS)
            transpose_rows(0, 1)
            transpose_rows(1, 1)
            hidden(0, 1)

            def slot(j, k, q):
                if not isinstance(j, int) or j + 2 < NJ:
                    transpose_rows((k + 2) % NW, q + 1 + (k + 2) // NW)
                if not isinstance(j, int) or j + 1 < NJ:
                    hidden((k + 1) % NW, q + 1 + (k + 1) // NW)
                outputs(j, k, q + 1)

            slots(pe, slot)

        @block.vector
        def _(dve):
            for n, (lo, hi) in enumerate(((0, S // P), (S // P, T))):
                for b in range(lo * P // S, hi * P // S):
                    dve.wait_ge(x_in[b], 16)
                with dve.Fori(lo, hi) as t:
                    nc.vector.bn_stats(one(t, 0, 6)(stats1), one(t)(x_sb)).then_inc(stats1_ready, 1)
                for t in range(lo, hi):
                    dve.wait_ge(stats1_ready, t + 1)
                    nc.vector.bn_aggr(mv1[:, t, :], stats1[:, t, :]).then_inc(mv1_ready, 1)
                dve.wait_ge(mv1_ready, hi)
                nc.vector.tensor_scalar(rstd1[:, lo:hi].unsqueeze(2), mv1[:, lo:hi, 1:2], EPS, None, ALU.add).then_inc(var1_ready, 1)
                if n == 0:
                    empty_some = [g for g in range(len(k_side)) if groups[g][3] == "dve"]
                    for g in empty_some:
                        dve.wait_ge(setup_ready, g + 1)
                        empty(nc.vector, groups[g][2], *groups[g][:2]).then_inc(setup_dve, 1)
                        if g == empty_some[1]:
                            dve.wait_ge(rstd1_ready, 1)
                            normalise_x(dve, 0, True)
                    copy_xT(dve, 0)
                    normalise_x(dve, 1)
                    head_max(dve, 0, 0)
                    head_max(dve, 0, 1)
                    copy_xT(dve, 1)
                    dve.wait_ge(bo_in, 16)
                    dve.wait_ge(tanh_ready, 1)
                    nc.vector.tensor_scalar(bo4[:, :, :], bo_row[:, :].unsqueeze(1).to_broadcast([1, B, D]), tg[0:1, 0:1],
                                            None, ALU.mult).then_inc(bo4_ready, 1)
                    for g in range(len(k_side), len(groups)):
                        if g == group("vwT", 0):
                            invert_sums(dve, 0, 0)
                        dve.wait_ge(setup_ready, g + 1)
                        empty(nc.vector, groups[g][2], *groups[g][:2]).then_inc(setup_dve, 1)
            dve.wait_ge(rstd1_ready, 2)
            dve.wait_ge(consts, CONSTS)

            def pair(j):
                r = j - 2
                if runs(j, lag=2):
                    copy_logits(dve, r)
                    max_logit(dve, r)
                if runs(j, ahead=2):
                    normalise_x(dve, j + 2)
                if runs(j, lag=2):
                    subtract_max(dve, r)
                if runs(j, ahead=1):
                    head_max(dve, j + 1, 0)
                if runs(j, lag=2):
                    mark_maxima(dve, r)
                    first_maximum(dve, r)
                    mark_expert(dve, r)
                    count_tokens(dve, r, 0)
                    count_tokens(dve, r, 1)
                invert_sums(dve, j, 1)
                if runs(j, lag=2):
                    place_row(dve, r)
                if runs(j, lag=1):
                    residual(dve, j - 1, 1)
                    aggregate_x2(dve, j - 1)
                if runs(j, lag=2):
                    send_payload(dve, r)
                if runs(j, ahead=1):
                    head_max(dve, j + 1, 1)
                if runs(j, ahead=2):
                    copy_xT(dve, j + 2)
                if runs(j, lag=1):
                    normalise_x2(dve, j - 1)
                    copy_x2T(dve, j - 1)
                if runs(j, ahead=1):
                    invert_sums(dve, j + 1, 0)
                residual(dve, j, 0)

            def route(r):
                copy_logits(dve, r)
                max_logit(dve, r)
                subtract_max(dve, r)
                mark_maxima(dve, r)
                first_maximum(dve, r)
                mark_expert(dve, r)
                count_tokens(dve, r, 0)
                count_tokens(dve, r, 1)

            pairs(dve, pair)
            r = NPAIR - 1
            route(r - 1)
            place_row(dve, r - 1)
            send_payload(dve, r - 1)
            residual(dve, r, 1)
            aggregate_x2(dve, r)
            normalise_x2(dve, r)
            copy_x2T(dve, r)
            route(r)
            place_row(dve, r)
            send_payload(dve, r)

            done = [0]

            def plan(step):
                step.then_inc(plan_step, 1)
                done[0] += 1
                dve.wait_ge(plan_step, done[0])

            def over_tiles(v):
                return v.unsqueeze(1).to_broadcast([P, NJ, E])

            by_tile = tile_no[:, :].unsqueeze(2).to_broadcast([P, NJ, E])
            dve.wait_ge(cnt_ready, 1)
            plan(nc.vector.tensor_copy(cnt[:, :], bank[:, MISC, 0:E]))
            plan(nc.vector.tensor_tensor(above[:, :, :], cnt[:, :].unsqueeze(2).to_broadcast([P, E, T]),
                                         tile_edge[:, :].unsqueeze(1).to_broadcast([P, E, T]), ALU.is_gt))
            plan(nc.vector.reduce_sum(ntiles[:, :], above[:, :, :], AX))
            plan(nc.vector.tensor_tensor_scan(cum_in[:, :], ones8[:, :], ntiles[:, :], 0.0, ALU.mult, ALU.add))
            plan(nc.vector.tensor_tensor(cum_ex[:, :], cum_in[:, :], ntiles[:, :], ALU.subtract))
            plan(nc.vector.tensor_tensor(sel[:, :, :], by_tile, over_tiles(cum_ex[:, :]), ALU.is_ge))
            plan(nc.vector.tensor_tensor(sel2[:, :, :], by_tile, over_tiles(cum_in[:, :]), ALU.is_lt))
            plan(nc.vector.tensor_tensor(sel[:, :, :], sel[:, :, :], sel2[:, :, :], ALU.mult))
            plan(nc.vector.tensor_tensor(picked[:, 0, :, :], sel[:, :, :], over_tiles(cum_ex[:, :]), ALU.mult))
            plan(nc.vector.tensor_tensor(picked[:, 1, :, :], sel[:, :, :], over_tiles(cnt[:, :]), ALU.mult))
            plan(nc.vector.tensor_tensor(picked[:, 2, :, :], sel[:, :, :], over_tiles(expert_no[:, :]), ALU.mult))
            plan(nc.vector.reduce_sum(pick[:, :, :], picked[:, :, :, :], AX))
            first_tile, count, expert = pick[:, 0, :], pick[:, 1, :], pick[:, 2, :]
            plan(nc.vector.tensor_tensor(wanted[:, :], tile_no[:, :], first_tile, ALU.subtract))
            plan(nc.vector.tensor_scalar(wanted[:, :], wanted[:, :], float(P), None, ALU.mult))
            plan(nc.vector.tensor_scalar(last_start[:, :], count, float(-P), 0.0, ALU.add, ALU.max))
            plan(nc.vector.tensor_tensor(start[:, :], wanted[:, :], last_start[:, :], ALU.min))
            plan(nc.vector.scalar_tensor_tensor(row_f[:, :], expert, float(REGION), start[:, :], ALU.mult, ALU.add))
            plan(nc.vector.tensor_copy(where_i[:, :, 0:1], row_f[:, :].unsqueeze(2)))
            plan(nc.vector.tensor_scalar(where_i[:, :, 1:2], expert.unsqueeze(2), float(P), None, ALU.mult))
            plan(nc.vector.tensor_scalar(w2_at_i[:, :], expert, float(FC * D), None, ALU.mult))
            plan(nc.vector.tensor_scalar(b2_at_i[:, :], expert, float(D), None, ALU.mult))
            plan(nc.vector.tensor_tensor(low[:, :], wanted[:, :], start[:, :], ALU.subtract))
            plan(nc.vector.tensor_tensor(high[:, :], count, start[:, :], ALU.subtract))
            plan(nc.vector.tensor_scalar(low[:, :], low[:, :], part_no[:, :], None, ALU.is_le))
            plan(nc.vector.tensor_scalar(high[:, :], high[:, :], part_no[:, :], None, ALU.is_gt))
            plan(nc.vector.tensor_tensor(drop[:, :], low[:, :], high[:, :], ALU.mult))
            plan(nc.vector.tensor_scalar(drop[:, :], drop[:, :], -DROP, DROP, ALU.mult, ALU.add))
            assert done[0] == PLAN_STEPS

            def erow(j, lo, hi):
                return one(j, lo, hi)(erows)

            def normalise_rows(j, k, uses):
                dve.wait_ge(erows_in[k], 16 * uses)
                if not (k < 2 and isinstance(uses, int) and uses < 2):
                    dve.wait_ge(exT_psum[(k - 2) % NW], uses - (k < 2))
                nc.vector.tensor_scalar(exn[:, k % 2, :], erow(j, 0, D), erow(j, MEAN, MEAN + 1), erow(j, RSTD, RSTD + 1),
                                        ALU.subtract, ALU.mult).then_inc(exn_ready[k], 1)

            def add_b1(k, uses):
                dve.wait_ge(h_ready[k], uses)
                if not (k < 2 and isinstance(uses, int) and uses < 2):
                    dve.wait_ge(hid_ready[(k - 2) % NW], uses - (k < 2))
                nc.vector.tensor_tensor(hbias[:, k % 2, :, :], bank[:, 2 + k % 2, :].rearrange("p (c k) -> p c k", c=FC),
                                        w1_sb[:, k, F:F + FC].unsqueeze(2).to_broadcast([P, FC, P]),
                                        ALU.add).then_inc(hbias_ready[k], 1)

            def finish(j, k, uses):
                b2_at = dve.value_load(b2_at_i[0:1, bass.ds(j, 1)], min_val=0, max_val=(E - 1) * D)
                if not (isinstance(uses, int) and uses < 2):
                    dve.wait_ge(stored[k], 16 * (uses - 1))
                nc.vector.tensor_scalar(token_i[:, k:k + 1], erow(j, TOKEN, TOKEN + 1), drop[:, bass.ds(j, 1)], None,
                                        ALU.add).then_inc(token_ready[k], 1)
                dve.wait_ge(y_ready[k], uses)
                nc.vector.tensor_tensor(ybias[:, k % 2, :], bank[:, 4 + k % 2, 0:D], b2_bc[:, bass.ds(b2_at, D)],
                                        ALU.add).then_inc(ybias_ready[k], 1)
                dve.wait_ge(ybias_ready[k], uses)
                nc.vector.scalar_tensor_tensor(eout[:, k, :], ybias[:, k % 2, :], erow(j, GATE, GATE + 1), erow(j, 0, D),
                                               ALU.mult, ALU.add).then_inc(eout_ready[k], 1)

            def slot(j, k, q):
                whole = not isinstance(j, int)
                if whole or j >= 1:
                    finish(j - 1, (k - 1) % NW, q + 1 - (k < 1))
                if whole or j + 3 < NJ:
                    normalise_rows(j + 3, (k + 3) % NW, q + 1 + (k + 3) // NW)
                if whole or j + 1 < NJ:
                    add_b1((k + 1) % NW, q + 1 + (k + 1) // NW)

            dve.wait_ge(b2_in, 16)
            for k in range(3):
                normalise_rows(k, k, 1)
            add_b1(0, 1)
            slots(dve, slot)
            finish(NJ - 1, (NJ - 1) % NW, (NJ - 1) // NW + 1)


PLAN_STEPS = 27
CONSTS = 14


_INS = ['x', 'ctx_t', 'g_xattn', 'g_ffn', 'Wq_t', 'L0_xattn_Wk', 'L0_xattn_Wv', 'L0_xattn_Wo', 'L0_xattn_bo',
        'L0_ffn_Wr', 'W1b1', 'L0_ffn_W2', 'L0_ffn_b2']
_OUTS = [((4, 512, 128), 'float32')]


def kernel(**inputs):
    import numpy as _np
    import concourse.bacc as _bacc
    from concourse import mybir as _mybir
    from concourse.bass_utils import run_bass_kernel_spmd as _run

    b1 = _np.asarray(inputs['L0_ffn_b1'])
    laid = dict(inputs)
    laid['ctx_t'] = _np.asarray(inputs['ctx_768']).transpose(2, 0, 1)
    laid['Wq_t'] = _np.asarray(inputs['L0_xattn_Wq']).T
    laid['W1b1'] = _np.concatenate(
        [_np.asarray(inputs['L0_ffn_W1']), b1.reshape(b1.shape[0], -1, 128).transpose(0, 2, 1)], axis=2)

    nc = _bacc.Bacc("TRN2", target_bir_lowering=False, num_devices=1)
    arrays, args = {}, []
    for name in _INS:
        a = _np.ascontiguousarray(laid[name])
        arrays[f"in_{name}_dram"] = a
        args.append(nc.dram_tensor(f"in_{name}_dram", a.shape, _mybir.dt.from_np(a.dtype), kind="ExternalInput").ap())
    for i, (shape, dtype) in enumerate(_OUTS):
        dt = _mybir.dt.from_np(_np.dtype(dtype))
        args.append(nc.dram_tensor(f"out_{i}_dram", shape, dt, kind="ExternalOutput").ap())
    flamingo_block(nc, *args)
    r = _run(nc, [arrays], core_ids=[0])
    got = tuple(r.results[0][f"out_{i}_dram"] for i in range(len(_OUTS)))
    return got[0]
```

```python
from contextlib import ExitStack

import concourse.bass as bass
from concourse import mybir

F32 = mybir.dt.float32
BF16 = mybir.dt.bfloat16
I32 = mybir.dt.int32
ALU = mybir.AluOpType
ACT = mybir.ActivationFunctionType
AX = mybir.AxisListType.X

P = 128
EPS = 1e-5


def flamingo_block(nc, x, ctx_t, g_xattn, g_ffn, Wq_t, Wk_t, Wv_t, Wo, bo, Wr, W1b1, W2, b2, out):
    B, S, D = x.shape
    C, _, L = ctx_t.shape
    INNER = Wq_t.shape[0]
    DH = 64
    H = INNER // DH
    E, F, _ = W2.shape
    assert W1b1.shape == (E, P, F + F // P)
    T = B * S // P
    NPAIR = T // 2
    PAIRS_PER_BATCH = S // P // 2
    HC = INNER // P
    HPC = P // DH
    FC = F // P
    HL = H * L
    HALF = HL // 2
    NCH = -(-HL // P)
    LASTC = HL - (NCH - 1) * P
    BL = B * L
    SCALE = float(DH) ** -0.5
    NTOK = B * S
    REGION = NTOK
    NJ = T + E - 1
    ROW = D + 4
    MEAN, RSTD, GATE, TOKEN = D, D + 1, D + 2, D + 3
    NW = 6
    DROP = float(2 * NTOK)
    assert D == P and HPC == 2 and HC * D == 512 and LASTC < P

    x_rows = x.rearrange("b s d -> (b s) d")
    out_rows = out.rearrange("b s d -> (b s) d")
    x_tiles = x_rows.rearrange("(t p) d -> p t d", p=P)
    scratch = nc.dram_tensor("expert_rows", [E * REGION, ROW], F32, kind="Internal").ap()

    with ExitStack() as es:
        def sb(name, shape, dt=F32):
            return es.enter_context(nc.sbuf_tensor(name, shape, dt))

        def sem(name):
            return es.enter_context(nc.semaphore(name))

        ctxT = sb("ctxT", [C, BL])
        wqT = sb("wqT", [P, HC, P])
        wkT = sb("wkT", [P, HC, C])
        wvT = sb("wvT", [P, HC, C])
        wo_sb = sb("wo_sb", [P, HC, D])
        qk = sb("qk", [C, H, D])
        vo = sb("vo", [C, H, D])
        A = sb("A", [P, B * HL])
        vwT = sb("vwT", [P, B, HL])
        vw = sb("vw", [P, B, NCH, D])
        wr_sb = sb("wr_sb", [P, E])
        w2_sb = sb("w2_sb", [P, E * FC * D])
        b2_bc = sb("b2_bc", [P, E * D])
        gates = sb("gates", [P, 2])
        tg = sb("tg", [P, 2])
        bo_row = sb("bo_row", [1, D])
        bo4 = sb("bo4", [1, B, D])
        ident = sb("ident", [P, P])
        tri = sb("tri", [P, P], BF16)
        ones_bf = sb("ones_bf", [P, P], BF16)
        rev = sb("rev", [P, E])
        region_at = sb("region_at", [P, E], BF16)
        ones8 = sb("ones8", [P, E])
        tile_edge = sb("tile_edge", [P, T])
        tile_no = sb("tile_no", [P, NJ])
        tile_row = sb("tile_row", [P, NJ])
        part_no = sb("part_no", [P, 1])
        gelu_warm = sb("gelu_warm", [P, 1])
        pad = sb("pad", [P, ROW])
        x_sb = sb("x_sb", [P, T, D])
        stats1 = sb("stats1", [P, T, 6])
        mv1 = sb("mv1", [P, T, 2])
        rstd1 = sb("rstd1", [P, T])
        xn = sb("xn", [P, 2, D])
        xnT = sb("xnT", [P, 2, P])
        negmax = sb("negmax", [P, 2, H])
        expsum = sb("expsum", [P, 2, H])
        rsum = sb("rsum", [P, 2, H])
        probs = sb("probs", [P, 2, HL + 1])
        probsT = sb("probsT", [P, 2, NCH, P])
        rows = sb("rows", [P, T, ROW])
        stats2 = sb("stats2", [P, 2, 6])
        mv2 = sb("mv2", [P, 2, 2])
        var2 = sb("var2", [P, 2])
        xn2 = sb("xn2", [P, 2, D])
        eps = sb("eps", [P, 2])
        minus_half = sb("minus_half", [P, T])
        xn2T = sb("xn2T", [P, 2, P])
        neg_lmax = sb("neg_lmax", [P, 2])
        below_max = sb("below_max", [P, 2, E])
        is_max = sb("is_max", [P, 2, E])
        first_max = sb("first_max", [P, 2])
        onehot = sb("onehot", [P, 2, E], BF16)
        running = sb("running", [P, T + 1, E], BF16)
        lexp = sb("lexp", [P, 2, E])
        lsum = sb("lsum", [P, 2])
        place = sb("place", [P, 2, E])
        SPARE, LAST = 2, 4
        place_i = sb("place_i", [P, LAST + 2], I32)
        payload = sb("payload", [P, LAST + 2, ROW])
        cnt = sb("cnt", [P, E])
        above = sb("above", [P, E, T])
        ntiles = sb("ntiles", [P, E])
        cum_in = sb("cum_in", [P, E])
        deltas = sb("deltas", [P, 3, E - 1])
        passed = sb("passed", [P, NJ, E - 1])
        picked = sb("picked", [P, 3, NJ, E - 1])
        pick = sb("pick", [P, 3, NJ])
        wanted = sb("wanted", [P, NJ])
        first_free = sb("first_free", [P, 1])
        last_start = sb("last_start", [P, NJ])
        start = sb("start", [P, NJ])
        low = sb("low", [P, NJ])
        high = sb("high", [P, NJ])
        not_below = sb("not_below", [P, NJ])
        own = sb("own", [P, NJ])
        where_i = sb("where_i", [P, 2, NJ], I32)
        w2_at_i = sb("w2_at_i", [P, NJ], I32)
        b2_at_i = sb("b2_at_i", [P, NJ], I32)
        drop = sb("drop", [P, NJ])
        erows = sb("erows", [P, NW, ROW])
        exn = sb("exn", [P, 2, D])
        exT = sb("exT", [P, 2, P])
        w1_sb = sb("w1_sb", [P, NW, F + FC])
        hbias = sb("hbias", [P, 2, FC, P])
        hid = sb("hid", [P, 2, FC, P])
        ybias = sb("ybias", [P, 2, D])
        eout = sb("eout", [P, NW, D])
        token_i = sb("token_i", [P, NW], I32)

        table_end = {w2_at_i.name: (E - 1) * FC * D, b2_at_i.name: (E - 1) * D}
        BOUNDED = "the plan keeps every tile inside its expert's region and experts between 0 and E - 1"

        bank = es.enter_context(nc.psum_tensor("bank", [P, 8, 512], F32))
        PT0, PT1, ATT, MISC = 4, 5, 6, 7

        ctx_in, wq_in, wk_in, wv_in, wo_in = (sem(n) for n in ("ctx_in", "wq_in", "wk_in", "wv_in", "wo_in"))
        x_in = [sem(f"x_in{b}") for b in range(B)]
        gates_in, wr_in, bo_in, b2_in, w2_in = (sem(n) for n in ("gates_in", "wr_in", "bo_in", "b2_in", "w2_in"))
        pads_out, bias_row_in = sem("pads_out"), sem("bias_row_in")

        def sems(*names):
            return [sem(n) for n in names]

        def sem2(name):
            return [sem(f"{name}{s}") for s in range(2)]

        def semk(name):
            return [sem(f"{name}{k}") for k in range(NW)]

        memsets, consts, setup_ready, setup_act, setup_dve, tanh_ready, bo4_ready, b2_scaled = sems(
            "memsets", "consts", "setup_ready", "setup_act", "setup_dve", "tanh_ready", "bo4_ready", "b2_scaled")
        stats1_ready, mv1_ready, var1_ready, rstd1_ready = sems("stats1_ready", "mv1_ready", "var1_ready", "rstd1_ready")
        xn_ready, xT_ready, xnT_ready = sems("xn_ready", "xT_ready", "xnT_ready")
        scores_ready, max_ready, exp_ready = sem2("scores_ready"), sem2("max_ready"), sem2("exp_ready")
        rsum_ready, probs_ready = sem2("rsum_ready"), sem2("probs_ready")
        pT_ready, probsT_ready = sem2("pT_ready"), sem2("probsT_ready")
        attn_ready, resid_ready, stats2_ready = sem2("attn_ready"), sem2("resid_ready"), sem2("stats2_ready")
        mv2_ready, var2_ready, rstd2_ready, stats_in_rows, xn2_ready, x2T_ready, xn2T_ready = sems(
            "mv2_ready", "var2_ready", "rstd2_ready", "stats_in_rows", "xn2_ready", "x2T_ready", "xn2T_ready")
        logits_ready, neg_lmax_ready, below_ready, marks_ready, first_ready, onehot_ready = sems(
            "logits_ready", "neg_lmax_ready", "below_ready", "marks_ready", "first_ready", "onehot_ready")
        running_ready, lexp_ready = sem2("running_ready"), sem("lexp_ready")
        lsum_ready, gate_ready = sems("lsum_ready", "gate_ready")
        rank_ready, rank_read = sems("rank_ready", "rank_read")
        payload_ready = sem2("payload_ready")
        scattered = sem2("scattered")
        cnt_ready, plan_step = sem("cnt_ready"), sem("plan_step")
        erows_in, w1_in = semk("erows_in"), semk("w1_in")
        exn_ready, exT_psum, exT_ready = semk("exn_ready"), semk("exT_psum"), semk("exT_ready")
        h_ready, hbias_ready, hid_ready = semk("h_ready"), semk("hbias_ready"), semk("hid_ready")
        y_ready, ybias_ready, eout_ready, stored = semk("y_ready"), semk("ybias_ready"), semk("eout_ready"), semk("stored")

        HPB = H // HPC
        k_side = [("qk", i, i, ("dve", "act")[i % 2]) for i in range(HPC)]
        k_side += [("A", h, (2 + h) % 8, ("dve", "act")[h % 2]) for h in range(H)]
        v_side = [("vo", i, 4 + i, "dve") for i in range(HPC)]
        v_side += [("vwT", h, (PT0, PT1, ATT, MISC, PT0, ATT, MISC, ATT)[h], "dve") for h in range(H)]
        v_side += [("vw_last", 0, MISC, "dve")]
        v_side += [("vw", b, (ATT, PT0, MISC, MISC)[b], "dve") for b in range(B)]
        groups = k_side + v_side

        def emptied(eng, n):
            who = groups[n][3]
            count = sum(1 for g in groups[:n + 1] if g[3] == who)
            eng.wait_ge(setup_act if who == "act" else setup_dve, count)

        def group(what, index):
            return next(n for n, g in enumerate(groups) if g[:2] == (what, index))

        LATE = group("vwT", 5)
        LATER = group("vw", 3)
        assert len(groups) == LATER + 1 and H == 8 and B == 4 and PAIRS_PER_BATCH == 2

        def last_in_bank(b, before):
            return max((n for n, g in enumerate(groups[:before]) if g[2] == b), default=None)

        def empty(eng, src_bank, what, i):
            act = eng is nc.scalar

            def copy(dst, src, scale=None):
                if act:
                    return nc.scalar.activation(dst, src, ACT.Copy, scale=1.0 if scale is None else scale)
                if scale is None:
                    return nc.vector.tensor_copy(dst, src)
                return nc.vector.tensor_scalar(dst, src, scale, None, ALU.mult)

            per_b = bank[:, src_bank, 0:BL].rearrange("p (b l) -> p b l", b=B)
            if what == "qk":
                return copy(qk[:, i * HPB:(i + 1) * HPB, :].rearrange("c h d -> c (h d)"), bank[0:C, src_bank, :], SCALE)
            if what == "A":
                return copy(A[:, :].rearrange("p (b h l) -> p b h l", b=B, h=H)[:, :, i, :], per_b)
            if what == "vo":
                return copy(vo[:, i * HPB:(i + 1) * HPB, :].rearrange("c h d -> c (h d)"), bank[0:C, src_bank, :], tg[0:C, 0:1])
            if what == "vwT":
                return copy(vwT[:, :, i * L:(i + 1) * L], per_b)
            if what == "vw":
                return copy(vw[:, i, 0:NCH - 1, :].rearrange("p c d -> p (c d)"), bank[:, src_bank, :])
            return copy(vw[0:LASTC, :, NCH - 1, :], bank[0:LASTC, src_bank, :].rearrange("p (b d) -> p b d", b=B))

        def fixed_wait(eng):
            eng.wait_ge(consts, 1)

        def one(t, lo=0, hi=D):
            return lambda tensor: tensor[:, bass.ds(t, 1), lo:hi].rearrange("p o d -> p (o d)")

        LOOP = (4, NPAIR - 2)

        def pairs(eng, pair):
            for j in range(LOOP[0]):
                pair(j)
            with eng.Fori(*LOOP) as j:
                pair(j)
            pair(NPAIR - 2)
            pair(NPAIR - 1)

        def runs(j, lag=0, ahead=0):
            return not isinstance(j, int) or (j >= lag and j + ahead < NPAIR)

        def normalise_x(dve, p, first=False):
            if not first:
                dve.wait_ge(xT_ready, p)
            for i in range(2):
                step = nc.vector.tensor_scalar(xn[:, i, :], one(2 * p + i)(x_sb), one(2 * p + i, 0, 1)(mv1),
                                               rstd1[:, bass.ds(2 * p + i, 1)], ALU.subtract, ALU.mult)
            step.then_inc(xn_ready, 1)

        def copy_xT(dve, p):
            dve.wait_ge(xT_ready, p + 1)
            nc.vector.tensor_copy(xnT[:, :, :].rearrange("p i k -> p (i k)"), bank[:, MISC, 0:2 * P]).then_inc(xnT_ready, 1)

        def head_max(dve, p, s):
            dve.wait_ge(scores_ready[s], p + 1)
            nc.vector.tensor_reduce(negmax[:, s, :].rearrange("p (b h) -> p b h", b=2),
                                    bank[:, 2 * s:2 * s + 2, 0:HALF].rearrange("p b (h l) -> p b h l", l=L),
                                    AX, ALU.max, negate=True).then_inc(max_ready[s], 1)

        def invert_sums(dve, p, s):
            dve.wait_ge(exp_ready[s], p + 1)
            nc.vector.reciprocal(rsum[:, s, :], expsum[:, s, :]).then_inc(rsum_ready[s], 1)

        def residual(dve, p, s):
            dve.wait_ge(attn_ready[s], p + 1)
            nc.vector.tensor_tensor(one(2 * p + s)(rows), bank[:, ATT, 0:D], one(2 * p + s)(x_sb), ALU.add)\
                .then_inc(resid_ready[s], 1)

        def residual_stats(dve, p, s):
            fixed_wait(dve)
            dve.wait_ge(resid_ready[s], p + 1)
            nc.vector.bn_stats(stats2[:, s, :], one(2 * p + s)(rows)).then_inc(stats2_ready[s], 1)

        def aggregate_x2(dve, r):
            for i in range(2):
                fixed_wait(dve)
                dve.wait_ge(stats2_ready[i], r + 1)
                step = nc.vector.bn_aggr(mv2[:, i, :], stats2[:, i, :])
            step.then_inc(mv2_ready, 1)

        def normalise_x2(dve, r):
            dve.wait_ge(rstd2_ready, r + 1)
            for i in range(2):
                step = nc.vector.tensor_scalar(xn2[:, i, :], one(2 * r + i)(rows), mv2[:, i, 0:1], mv2[:, i, 1:2],
                                               ALU.subtract, ALU.mult)
            step.then_inc(xn2_ready, 1)
            nc.vector.tensor_copy(rows[:, bass.ds(2 * r, 2), MEAN:RSTD + 1], mv2[:, :, :]).then_inc(stats_in_rows, 1)

        def copy_x2T(dve, r):
            dve.wait_ge(x2T_ready, r + 1)
            nc.vector.tensor_copy(xn2T[:, :, :].rearrange("p i k -> p (i k)"), bank[:, MISC, 0:2 * P]).then_inc(xn2T_ready, 1)

        def by_expert(v):
            return v.unsqueeze(1).to_broadcast([P, 2, E])

        def by_token(v):
            return v.unsqueeze(2).to_broadcast([P, 2, E])

        def router_logits():
            return bank[:, MISC, 0:2 * E].rearrange("p (i e) -> p i e", i=2)

        def max_logit(dve, r):
            dve.wait_ge(logits_ready, r + 1)
            nc.vector.tensor_reduce(neg_lmax[:, :], router_logits(), AX, ALU.max, negate=True).then_inc(neg_lmax_ready, 1)

        def subtract_max(dve, r):
            dve.wait_ge(neg_lmax_ready, r + 1)
            if not (isinstance(r, int) and r < 1):
                dve.wait_ge(lexp_ready, r)
            nc.vector.tensor_tensor(below_max[:, :, :], router_logits(), by_token(neg_lmax[:, :]), ALU.add).then_inc(below_ready, 1)

        def mark_maxima(dve, r):
            dve.wait_ge(below_ready, r + 1)
            nc.vector.scalar_tensor_tensor(is_max[:, :, :], below_max[:, :, :], 0.0, by_expert(rev[:, :]),
                                           ALU.is_equal, ALU.mult).then_inc(marks_ready, 1)

        def first_maximum(dve, r):
            dve.wait_ge(marks_ready, r + 1)
            nc.vector.tensor_reduce(first_max[:, :], is_max[:, :, :], AX, ALU.max).then_inc(first_ready, 1)

        def mark_expert(dve, r):
            dve.wait_ge(first_ready, r + 1)
            nc.vector.tensor_tensor(onehot[:, :, :], by_expert(rev[:, :]), by_token(first_max[:, :]), ALU.is_equal)\
                .then_inc(onehot_ready, 1)

        def count_tokens(dve, r, i):
            dve.wait_ge(running_ready[0], r + 1) if i else dve.wait_ge(onehot_ready, r + 1)
            nc.vector.tensor_tensor(one(2 * r + i + 1, 0, E)(running), one(2 * r + i, 0, E)(running),
                                    onehot[:, i, :], ALU.add).then_inc(running_ready[i], 1)

        def own_rank(dve, r, b=MISC):
            dve.wait_ge(rank_ready, r + 1)
            nc.vector.tensor_tensor(place[:, :, :], bank[:, b, 0:2 * E].rearrange("p (i e) -> p i e", i=2),
                                    onehot[:, :, :], ALU.mult).then_inc(rank_read, 1)

        def sum_exps(dve, r):
            dve.wait_ge(lexp_ready, r + 1)
            nc.vector.reduce_sum(lsum[:, :], lexp[:, :, :], AX).then_inc(lsum_ready, 1)

        def gate(dve, r):
            dve.wait_ge(lsum_ready, r + 1)
            nc.vector.reciprocal(rows[:, bass.ds(2 * r, 2), GATE:GATE + 1], lsum[:, :].unsqueeze(2)).then_inc(gate_ready, 1)

        def send_payload(dve, r, i, buf=0):
            if buf == 0 and not (isinstance(r, int) and r < 1):
                dve.wait_ge(scattered[i], 16 * r)
            dve.wait_ge(rank_read, r + 1)
            nc.vector.tensor_reduce(place_i[:, buf + i:buf + i + 1], place[:, i, :], AX, ALU.max)
            dve.wait_ge(gate_ready, r + 1)
            dve.wait_ge(stats_in_rows, r + 1)
            nc.vector.tensor_copy(payload[:, buf + i, :], one(2 * r + i, 0, ROW)(rows)).then_inc(payload_ready[i], 1)

        def slots(eng, slot, table=None, lag=0):
            def three(j, k, q, n=3):
                at = [None] * n
                skip = lag if isinstance(j, int) and j < lag else 0
                if table is not None:
                    _, at[skip:] = nc.values_load_multi_w_load_instructions(
                        table[0:1, bass.ds(j + skip - lag, n - skip)], engines=[eng.engine], min_val=0,
                        max_val=table_end[table.name], skip_runtime_bounds_check_because=BOUNDED)
                for i in range(n):
                    slot(j + i, (k + i) % NW, q + (k + i) // NW, at[i])

            def peeled(lo, hi):
                for j in range(lo, hi, 3):
                    three(j, j % NW, j // NW, min(3, hi - j))

            peeled(0, NW + 1)
            with eng.Fori(1, (NJ - 4) // NW) as q:
                for k in range(1, NW + 1, 3):
                    three(NW * q + k, k, q)
            peeled((NJ - 4) // NW * NW + 1, NJ)

        block = es.enter_context(nc.Block())

        @block.sync
        def _(sp):
            per = S // P
            sp.dma_start(wkT[:, :, :], Wk_t.rearrange("(i p) c -> p i c", p=P)).then_inc(wk_in, 16)
            sp.dma_start(ctxT[:, :], ctx_t.rearrange("c b l -> c (b l)")).then_inc(ctx_in, 16)
            sp.dma_start(x_sb[:, 0:per, :], x_tiles[:, 0:per, :]).then_inc(x_in[0], 16)
            sp.dma_start(wvT[:, :, :], Wv_t.rearrange("(i p) c -> p i c", p=P)).then_inc(wv_in, 16)
            sp.dma_start(wo_sb[:, :, :], Wo.rearrange("(c p) d -> p c d", p=P)).then_inc(wo_in, 16)
            for b in range(1, B):
                sp.dma_start(x_sb[:, b * per:(b + 1) * per, :], x_tiles[:, b * per:(b + 1) * per, :]).then_inc(x_in[b], 16)
            sp.wait_ge(memsets, 5)
            for e in range(E):
                sp.dma_start(scratch[e * REGION:e * REGION + P, :], pad[:, :]).then_inc(pads_out, 16)
            sp.wait_ge(bo4_ready, 1)
            sp.dma_start(vw[LASTC:LASTC + 1, :, NCH - 1, :], bo4[:, :, :]).then_inc(bias_row_in, 16)
            sp.dma_start(b2_bc[:, :], b2.rearrange("(o e) d -> o (e d)", o=1).partition_broadcast(P)).then_inc(b2_in, 16)
            sp.dma_start(w2_sb[:, :].rearrange("p (e c d) -> p e c d", e=E, c=FC),
                         W2.rearrange("e (c p) d -> p e c d", p=P)).then_inc(w2_in, 16)

            def where(j, what, n):
                _, at = nc.values_load_multi_w_load_instructions(
                    where_i[0:1, what:what + 1, bass.ds(j, n)].rearrange("p o n -> p (o n)"), engines=[sp.engine],
                    min_val=0, max_val=(E * REGION - P, (E - 1) * P)[what], skip_runtime_bounds_check_because=BOUNDED)
                return at

            def load_w1(k, at):
                sp.dma_start(w1_sb[:, k, :], W1b1.rearrange("e p f -> (e p) f")[bass.ds(at, P), :]).then_inc(w1_in[k], 16)

            def load_rows(k, at):
                sp.dma_start(erows[:, k, :], scratch[bass.ds(at, P), :]).then_inc(erows_in[k], 16)

            def load_three(j, k, q, n=3):
                w1_at, rows_at = where(j, 1, n), where(j, 0, n)
                for i in range(n):
                    sp.wait_ge(hbias_ready[k + i], q)
                    load_w1(k + i, w1_at[i])
                    sp.wait_ge(eout_ready[k + i], q)
                    load_rows(k + i, rows_at[i])

            sp.wait_ge(plan_step, EXPERTS_PLANNED)
            w1_at = where(0, 1, NW)
            load_w1(0, w1_at[0])
            sp.wait_ge(plan_step, ROWS_PLANNED)
            rows_at = where(0, 0, NW)
            for i in range(2):
                sp.wait_ge(scattered[i], 16 * NPAIR)
            load_rows(0, rows_at[0])
            for k in range(1, NW):
                load_rows(k, rows_at[k])
                load_w1(k, w1_at[k])
            with sp.Fori(1, NJ // NW) as q:
                for k in range(0, NW, 3):
                    load_three(NW * q + k, k, q)
            for j in range(NJ // NW * NW, NJ, 3):
                load_three(j, j % NW, j // NW, min(3, NJ - j))

        @block.gpsimd
        def _(pool):
            nc.gpsimd.memset(ones_bf[:, :], 1.0).then_inc(memsets, 1)
            nc.gpsimd.memset(ident[:, :], 0.0).then_inc(memsets, 1)
            nc.gpsimd.memset(tri[:, :], 1.0).then_inc(memsets, 1)
            nc.gpsimd.memset(region_at[:, :], 0.0).then_inc(memsets, 1)
            nc.gpsimd.memset(pad[:, :], 0.0).then_inc(memsets, 1)
            nc.gpsimd.memset(minus_half[:, :], -0.5).then_inc(consts, 1)
            nc.gpsimd.memset(eps[:, :], EPS).then_inc(consts, 1)
            pool.wait_ge(memsets, 4)
            nc.gpsimd.affine_select(out=ident[:, :], in_=ident[:, :], compare_op=ALU.not_equal, fill=1.0,
                                    base=0, pattern=[[-1, P]], channel_multiplier=1).then_inc(consts, 1)
            nc.gpsimd.affine_select(out=tri[:, :], in_=tri[:, :], compare_op=ALU.is_gt, fill=0.0,
                                    base=0, pattern=[[1, P]], channel_multiplier=-1).then_inc(consts, 1)

            def count_up(dst, step, n, base=0, per_partition=0):
                nc.gpsimd.iota(dst, [[step, n]], base=base, channel_multiplier=per_partition,
                               allow_small_or_imprecise_dtypes=True).then_inc(consts, 1)

            count_up(rev[:, :], -1, E, base=E)
            count_up(region_at[0:1, :], REGION, E)
            count_up(tile_edge[:, :], P, T)
            count_up(tile_no[:, :], 1, NJ)
            count_up(tile_row[:, :], P, NJ)
            count_up(part_no[:, :], 0, 1, per_partition=1)
            count_up(rows[:, :, TOKEN:TOKEN + 1].rearrange("p t o -> p (t o)"), P, T, per_partition=1)
            nc.gpsimd.memset(ones8[:, :], 1.0).then_inc(consts, 1)
            nc.gpsimd.memset(running[:, 0, :], 0.0).then_inc(consts, 1)
            nc.gpsimd.memset(probs[:, :, HL:HL + 1], 1.0).then_inc(consts, 1)
            pool.wait_ge(consts, CONSTS)
            for n, (lo, hi) in enumerate(((0, S // P), (S // P, T))):
                pool.wait_ge(var1_ready, n + 1)
                nc.gpsimd.tensor_tensor(rstd1[:, lo:hi], rstd1[:, lo:hi], minus_half[:, lo:hi], ALU.pow).then_inc(rstd1_ready, 1)

            def normalise(p, s):
                pool.wait_ge(rsum_ready[s], p + 1)
                v = probs[:, s, 0:HL].rearrange("p (h l) -> p h l", h=H)
                nc.gpsimd.tensor_tensor(v, v, rsum[:, s, :].unsqueeze(2).to_broadcast([P, H, L]), ALU.mult)\
                    .then_inc(probs_ready[s], 1)

            def invert_std(r):
                pool.wait_ge(mv2_ready, r + 1)
                nc.gpsimd.tensor_tensor(var2[:, :].unsqueeze(2), mv2[:, :, 1:2], eps[:, :].unsqueeze(2), ALU.add)\
                    .then_inc(var2_ready, 1)
                pool.wait_ge(var2_ready, r + 1)
                nc.gpsimd.tensor_tensor(mv2[:, :, 1:2], var2[:, :].unsqueeze(2), minus_half[:, 0:2].unsqueeze(2), ALU.pow)\
                    .then_inc(rstd2_ready, 1)

            def scatter(i, placed, buf=0):
                fixed_wait(pool)
                pool.wait_ge(payload_ready[i], placed)
                nc.gpsimd.indirect_dma_start(scratch, bass.IndirectOffsetOnAxis(place_i[:, buf + i:buf + i + 1], 0),
                                             payload[:, buf + i, :], None,
                                             bounds_check=E * REGION - 1, oob_is_err=False)\
                    .then_inc(scattered[i], 16)

            def pair(j, placed):
                normalise(j, 1)
                if runs(j, lag=3):
                    scatter(0, placed)
                if runs(j, lag=1):
                    invert_std(j - 1)
                if runs(j, ahead=1):
                    normalise(j + 1, 0)
                if runs(j, lag=3):
                    scatter(1, placed)
                if isinstance(j, int) and j == 1:
                    pool.wait_ge(b2_in, 16)
                    pool.wait_ge(tanh_ready, 1)
                    nc.gpsimd.tensor_tensor(b2_bc[:, :], b2_bc[:, :], tg[:, 1:2].to_broadcast([P, E * D]), ALU.mult)\
                        .then_inc(b2_scaled, 1)

            pool.wait_ge(pads_out, 16 * E)
            normalise(0, 0)
            for j in range(LOOP[0]):
                pair(j, j - 2)
            with pool.Fori(LOOP[0] - 2, LOOP[1] - 2) as placed:
                pair(placed + 2, placed)
            pair(NPAIR - 2, NPAIR - 4)
            pair(NPAIR - 1, NPAIR - 3)
            scatter(0, NPAIR - 2, SPARE)
            invert_std(NPAIR - 1)
            scatter(1, NPAIR - 2, SPARE)
            for i in range(2):
                scatter(i, NPAIR - 1)
            for i in range(2):
                scatter(i, NPAIR, LAST)

            def store(k, uses):
                fixed_wait(pool)
                pool.wait_ge(eout_ready[k], uses)
                nc.gpsimd.indirect_dma_start(out_rows, bass.IndirectOffsetOnAxis(token_i[:, k:k + 1], 0),
                                             eout[:, k, :], None, bounds_check=NTOK - 1, oob_is_err=False)\
                    .then_inc(stored[k], 16)

            with pool.Fori(1, NJ // NW + 1) as uses:
                for k in range(NW):
                    store(k, uses)
            for k in range(NJ % NW):
                store(k, NJ // NW + 1)
            for k in range(NW):
                pool.wait_ge(stored[k], 16 * len(range(k, NJ, NW)))

        @block.scalar
        def _(act):
            act.dma_start(wqT[:, :, :], Wq_t.rearrange("(c p) d -> p c d", p=P)).then_inc(wq_in, 16)
            act.dma_start(gates[:, 0:1], g_xattn.rearrange("(o g) -> o g", o=1).partition_broadcast(P)).then_inc(gates_in, 16)
            act.dma_start(gates[:, 1:2], g_ffn.rearrange("(o g) -> o g", o=1).partition_broadcast(P)).then_inc(gates_in, 16)
            act.dma_start(bo_row[:, :], bo.rearrange("(o d) -> o d", o=1)).then_inc(bo_in, 16)
            act.dma_start(wr_sb[:, :], Wr).then_inc(wr_in, 16)
            act.wait_ge(gates_in, 32)
            nc.scalar.activation(tg[:, :], gates[:, :], ACT.Tanh).then_inc(tanh_ready, 1)

            def exps(p, s):
                act.wait_ge(max_ready[s], p + 1)
                if not (isinstance(p, int) and p < 1):
                    act.wait_ge(pT_ready[s], p)
                for h in range(H):
                    src = bank[:, 2 * s + h // (H // 2), (h % (H // 2)) * L:(h % (H // 2) + 1) * L]
                    step = nc.scalar.activation(probs[:, s, h * L:(h + 1) * L], src, ACT.Exp,
                                                bias=negmax[:, s, h:h + 1], accum_out=expsum[:, s, h:h + 1])
                step.then_inc(exp_ready[s], 1)

            def copy_probsT(p, s):
                act.wait_ge(pT_ready[s], p + 1)
                nc.scalar.activation(probsT[:, s, 0:NCH - 1, :].rearrange("p c k -> p (c k)"),
                                     bank[:, PT0, :], ACT.Copy)
                nc.scalar.activation(probsT[0:LASTC + 1, s, NCH - 1, :], bank[0:LASTC + 1, PT1, 0:P], ACT.Copy)\
                    .then_inc(probsT_ready[s], 1)

            def router_exps(r):
                act.wait_ge(below_ready, r + 1)
                if not (isinstance(r, int) and r < 1):
                    act.wait_ge(lsum_ready, r)
                nc.scalar.activation(lexp[:, :, :].rearrange("p i e -> p (i e)"),
                                     below_max[:, :, :].rearrange("p i e -> p (i e)"), ACT.Exp).then_inc(lexp_ready, 1)

            def pair(j):
                exps(j, 1)
                copy_probsT(j, 0)
                if runs(j, ahead=1):
                    exps(j + 1, 0)
                if runs(j, lag=2):
                    router_exps(j - 2)
                copy_probsT(j, 1)

            for n, (what, i, b, who) in enumerate(groups):
                if who == "act":
                    act.wait_ge(setup_ready, n + 1)
                    empty(nc.scalar, b, what, i).then_inc(setup_act, 1)
            exps(0, 0)
            pairs(act, pair)
            router_exps(NPAIR - 2)
            router_exps(NPAIR - 1)
            nc.scalar.activation(gelu_warm[:, :], ident[:, 0:1], ACT.Gelu)

            def copy_rowsT(k, uses):
                act.wait_ge(exT_psum[k], uses)
                if not (k < 2 and isinstance(uses, int) and uses < 2):
                    act.wait_ge(h_ready[(k - 2) % NW], uses - (k < 2))
                nc.scalar.activation(exT[:, k % 2, :], bank[:, k % 2, 0:P], ACT.Copy).then_inc(exT_ready[k], 1)

            def gelu(k, uses):
                act.wait_ge(hbias_ready[k], uses)
                if not (k < 2 and isinstance(uses, int) and uses < 2):
                    act.wait_ge(y_ready[(k - 2) % NW], uses - (k < 2))
                nc.scalar.activation(hid[:, k % 2, :, :].rearrange("p c k -> p (c k)"),
                                     hbias[:, k % 2, :, :].rearrange("p c k -> p (c k)"), ACT.Gelu)\
                    .then_inc(hid_ready[k], 1)

            def slot(j, k, q, _):
                if not isinstance(j, int) or j + 2 < NJ:
                    copy_rowsT((k + 2) % NW, q + 1 + (k + 2) // NW)
                if not isinstance(j, int) or j + 1 < NJ:
                    gelu((k + 1) % NW, q + 1 + (k + 1) // NW)

            copy_rowsT(0, 1)
            copy_rowsT(1, 1)
            gelu(0, 1)
            slots(act, slot)

        @block.tensor
        def _(pe):
            def setup(lo, hi):
                for n in range(lo, hi):
                    what, i, b, _ = groups[n]
                    if (prev := last_in_bank(b, n)) is not None:
                        emptied(pe, prev)
                    if what in ("qk", "vo"):
                        pe.wait_ge(wk_in if what == "qk" else wv_in, 16)
                        pe.wait_ge(wq_in if what == "qk" else wo_in, 16)
                        w, m = (wkT, wqT) if what == "qk" else (wvT, wo_sb)
                        at = i * DH
                        for c in range(HC):
                            step = nc.tensor.matmul(bank[0:C, b, c * D:(c + 1) * D], w[at:at + DH, c, :], m[at:at + DH, c, :],
                                                    start=True, stop=True)
                    elif what in ("A", "vwT"):
                        emptied(pe, group("qk" if what == "A" else "vo", i % HPC))
                        pe.wait_ge(ctx_in, 16)
                        w = qk if what == "A" else vo
                        step = nc.tensor.matmul(bank[:, b, 0:BL], w[:, i % HPC * HPB + i // HPC, :], ctxT[:, :], start=True, stop=True)
                    elif what == "vw":
                        emptied(pe, group("vwT", H - 2))
                        emptied(pe, group("vwT", H - 1))
                        for c in range(NCH - 1):
                            step = nc.tensor.transpose(bank[:, b, c * P:(c + 1) * P], vwT[:, i, c * P:(c + 1) * P], ident[:, :])
                    else:
                        emptied(pe, group("vwT", H - 1))
                        for k in range(B):
                            step = nc.tensor.transpose(bank[0:LASTC, b, k * P:(k + 1) * P], vwT[:, k, (NCH - 1) * P:HL], ident[:, :])
                    step.then_inc(setup_ready, 1)

            def transpose_x(p, guard=None):
                pe.wait_ge(xn_ready, p + 1)
                if guard is not None:
                    pe.wait_ge(*guard)
                for i in range(2):
                    step = nc.tensor.transpose(bank[:, MISC, i * P:(i + 1) * P], xn[:, i, :], ident[:, :])
                step.then_inc(xT_ready, 1)

            def scores(p, s):
                pe.wait_ge(xnT_ready, p + 1)
                if not (isinstance(p, int) and p < 1):
                    pe.wait_ge(exp_ready[s], p)
                for half in range(2):
                    step = nc.tensor.matmul(bank[:, 2 * s + half, 0:HALF], xnT[:, s, :],
                                            A[:, bass.ds(p // PAIRS_PER_BATCH * HL + half * HALF, HALF)],
                                            start=True, stop=True)
                step.then_inc(scores_ready[s], 1)

            def transpose_probs(p, s):
                pe.wait_ge(probs_ready[s], p + 1)
                if isinstance(p, int) and p < 2 and s == 0:
                    emptied(pe, last_in_bank(PT0, (LATE, LATER)[p]))
                    emptied(pe, last_in_bank(PT1, (LATE, LATER)[p]))
                if not (isinstance(p, int) and p < 1 and s == 0):
                    pe.wait_ge(probsT_ready[1 - s], p + s)
                for c in range(NCH - 1):
                    nc.tensor.transpose(bank[:, PT0, c * P:(c + 1) * P], probs[:, s, c * P:(c + 1) * P], ident[:, :])
                nc.tensor.transpose(bank[0:LASTC + 1, PT1, 0:P], probs[:, s, (NCH - 1) * P:HL + 1], ident[:, :])\
                    .then_inc(pT_ready[s], 1)

            def attend(p, s):
                pe.wait_ge(probsT_ready[s], p + 1)
                if isinstance(p, int) and p < 1 and s == 0:
                    pe.wait_ge(bias_row_in, 16)
                    emptied(pe, group("vw_last", 0))
                    emptied(pe, group("vw", 0))
                    assert last_in_bank(ATT, len(groups)) == group("vw", 0)
                else:
                    pe.wait_ge(resid_ready[1 - s], p + s)
                if isinstance(p, int) and p == PAIRS_PER_BATCH and s == 0:
                    emptied(pe, group("vw", B - 1))
                for c in range(NCH):
                    k = P if c < NCH - 1 else LASTC + 1
                    step = nc.tensor.matmul(bank[:, ATT, 0:D], probsT[0:k, s, c, :],
                                            vw[0:k, bass.ds(p // PAIRS_PER_BATCH, 1), c, :].rearrange("p o d -> p (o d)"),
                                            start=c == 0, stop=c == NCH - 1)
                step.then_inc(attn_ready[s], 1)

            def transpose_x2(r, guard):
                pe.wait_ge(xn2_ready, r + 1)
                pe.wait_ge(*guard)
                for i in range(2):
                    step = nc.tensor.transpose(bank[:, MISC, i * P:(i + 1) * P], xn2[:, i, :], ident[:, :])
                step.then_inc(x2T_ready, 1)

            def router(r):
                pe.wait_ge(xn2T_ready, r + 1)
                pe.wait_ge(wr_in, 16)
                for i in range(2):
                    step = nc.tensor.matmul(bank[:, MISC, i * E:(i + 1) * E], xn2T[:, i, :], wr_sb[:, :], start=True, stop=True)
                step.then_inc(logits_ready, 1)

            def ranks(r, b=MISC):
                pe.wait_ge(onehot_ready, r + 1)
                pe.wait_ge(running_ready[0], r + 1)
                nc.tensor.matmul(bank[:, b, 0:2 * E], tri[:, :], onehot[:, :, :].rearrange("p i e -> p (i e)"),
                                 start=True, stop=False)
                nc.tensor.matmul(bank[:, b, 0:2 * E], ones_bf[:, :], region_at[:, :].unsqueeze(1).to_broadcast([P, 2, E]),
                                 start=False, stop=False)
                nc.tensor.matmul(bank[:, b, 0:2 * E], ones_bf[:, :],
                                 running[:, bass.ds(2 * r, 2), :].rearrange("p i e -> p (i e)"),
                                 start=False, stop=True).then_inc(rank_ready, 1)

            def pair(j):
                if runs(j, lag=3):
                    ranks_before(j)
                if isinstance(j, int) and j == 2:
                    pe.wait_ge(xnT_ready, j + 2)
                    setup(LATER, LATER + 1)
                if runs(j, ahead=1) and not (isinstance(j, int) and j == 1):
                    scores(j + 1, 0)
                if isinstance(j, int) and j == 2:
                    emptied(pe, LATER)
                if runs(j, lag=2):
                    transpose_x2(j - 2, (rank_read, j - 2) if runs(j, lag=3) else (xnT_ready, j + 2))
                transpose_probs(j, 0)
                if runs(j, lag=1):
                    attend(j - 1, 1)
                if runs(j, lag=2):
                    router(j - 2)
                if runs(j, ahead=1):
                    scores(j + 1, 1)
                if runs(j, ahead=2):
                    if isinstance(j, int) and j < 2:
                        emptied(pe, last_in_bank(MISC, (LATE, LATER)[j]))
                    transpose_x(j + 2, (below_ready, j - 1) if runs(j, lag=2) else (xnT_ready, j + 2))
                transpose_probs(j, 1)
                if isinstance(j, int) and j < 1:
                    setup(LATE, LATE + 1)
                    pe.wait_ge(xnT_ready, 3)
                    setup(LATE + 1, LATE + 3)
                    scores(j + 2, 0)
                    setup(LATE + 3, group("vw", 1))
                    pe.wait_ge(probsT_ready[1], 1)
                    setup(group("vw", 1), LATER)
                attend(j, 0)

            def ranks_before(j):
                if runs(j, ahead=1):
                    pe.wait_ge(xnT_ready, j + 2)
                ranks(j - 3)

            def warm_up(n):
                for _ in range(n):
                    nc.tensor.matmul(bank[:, 0, :], ones_bf[:, :], ones_bf[:, :].unsqueeze(1).to_broadcast([P, 4, P]),
                                     start=True, stop=True)

            pe.wait_ge(memsets, 1)
            warm_up(14)
            pe.wait_ge(consts, CONSTS)
            setup(0, len(k_side))
            emptied(pe, last_in_bank(MISC, len(k_side)))
            transpose_x(0)
            setup(len(k_side), len(k_side) + 1)
            for b in range(4):
                emptied(pe, last_in_bank(b, len(k_side)))
            emptied(pe, group("A", H - 1))
            emptied(pe, group("A", H - 2))
            scores(0, 0)
            setup(len(k_side) + 1, len(k_side) + HPC)
            scores(0, 1)
            transpose_x(1, (xnT_ready, 1))
            in_misc = group("vwT", 3)
            setup(len(k_side) + HPC, in_misc)
            pe.wait_ge(xnT_ready, 2)
            setup(in_misc, LATE)
            pairs(pe, pair)
            r = NPAIR - 1
            ranks_before(NPAIR)
            attend(r, 1)
            transpose_x2(r - 1, (rank_read, r - 1))
            router(r - 1)
            transpose_x2(r, (below_ready, r))
            ranks(r - 1, PT0)
            router(r)
            ranks(r)
            pe.wait_ge(running_ready[1], NPAIR)
            nc.tensor.matmul(bank[:, PT1, 0:E], ones_bf[:, :], running[:, T, :], start=True, stop=True).then_inc(cnt_ready, 1)
            warm_up(22)

            def transpose_rows(k, uses):
                pe.wait_ge(exn_ready[k], uses)
                if not (k < 2 and isinstance(uses, int) and uses < 2):
                    pe.wait_ge(exT_ready[(k - 2) % NW], uses - (k < 2))
                nc.tensor.transpose(bank[:, k % 2, 0:P], exn[:, k % 2, :], ident[:, :]).then_inc(exT_psum[k], 1)

            def hidden(k, uses):
                pe.wait_ge(exT_ready[k], uses)
                pe.wait_ge(w1_in[k], 16 * uses)
                if not (k < 2 and isinstance(uses, int) and uses < 2):
                    pe.wait_ge(hbias_ready[(k - 2) % NW], uses - (k < 2))
                for c in range(FC):
                    step = nc.tensor.matmul(bank[:, 2 + k % 2, c * P:(c + 1) * P], w1_sb[:, k, c * P:(c + 1) * P],
                                            exT[:, k % 2, :], start=True, stop=True)
                step.then_inc(h_ready[k], 1)

            def outputs(k, uses, w2_at):
                pe.wait_ge(hid_ready[k], uses)
                if not (k < 2 and isinstance(uses, int) and uses < 2):
                    pe.wait_ge(ybias_ready[(k - 2) % NW], uses - (k < 2))
                for c in range(FC):
                    step = nc.tensor.matmul(bank[:, 4 + k % 2, 0:D], hid[:, k % 2, c, :],
                                            w2_sb[:, bass.ds(w2_at + c * D, D)], start=c == 0, stop=c == FC - 1)
                step.then_inc(y_ready[k], 1)

            pe.wait_ge(w2_in, 16)
            pe.wait_ge(plan_step, PLAN_STEPS)
            transpose_rows(0, 1)
            transpose_rows(1, 1)
            hidden(0, 1)

            def slot(j, k, q, w2_at):
                if not isinstance(j, int) or j + 2 < NJ:
                    transpose_rows((k + 2) % NW, q + 1 + (k + 2) // NW)
                if not isinstance(j, int) or j + 1 < NJ:
                    hidden((k + 1) % NW, q + 1 + (k + 1) // NW)
                outputs(k, q + 1, w2_at)

            slots(pe, slot, w2_at_i)

        @block.vector
        def _(dve):
            def statistics(t):
                nc.vector.bn_stats(stats1[:, t, :], x_sb[:, t, :]).then_inc(stats1_ready, 1)

            def aggregate(lo, hi):
                for t in range(lo, hi):
                    dve.wait_ge(stats1_ready, t + 1)
                    nc.vector.bn_aggr(mv1[:, t, :], stats1[:, t, :]).then_inc(mv1_ready, 1)
                dve.wait_ge(mv1_ready, hi)
                nc.vector.tensor_scalar(rstd1[:, lo:hi].unsqueeze(2), mv1[:, lo:hi, 1:2], EPS, None, ALU.add)\
                    .then_inc(var1_ready, 1)

            def empty_group(g):
                dve.wait_ge(setup_ready, g + 1)
                empty(nc.vector, groups[g][2], *groups[g][:2]).then_inc(setup_dve, 1)

            TB = S // P
            dve.wait_ge(x_in[0], 16)
            for t in range(TB):
                statistics(t)
            aggregate(0, TB)
            k_dve = [g for g in range(len(k_side)) if groups[g][3] == "dve"]
            assert len(k_dve) == B + 1
            for n, g in enumerate(k_dve):
                empty_group(g)
                if n == 1:
                    dve.wait_ge(rstd1_ready, 1)
                    normalise_x(dve, 0, True)
                if n >= 1 and n < B:
                    dve.wait_ge(x_in[n], 16)
                    for t in range(n * TB, (n + 1) * TB):
                        statistics(t)
            copy_xT(dve, 0)
            normalise_x(dve, 1)
            vo = len(k_side)
            dve.wait_ge(tanh_ready, 1)
            empty_group(vo)
            head_max(dve, 0, 0)
            empty_group(vo + 1)
            aggregate(TB, T)
            copy_xT(dve, 1)
            head_max(dve, 0, 1)
            for g in range(vo + HPC, LATE):
                empty_group(g)
                if g == vo + HPC + 2:
                    invert_sums(dve, 0, 0)
            dve.wait_ge(bo_in, 16)
            nc.vector.tensor_scalar(bo4[:, :, :], bo_row[:, :].unsqueeze(1).to_broadcast([1, B, D]), tg[0:1, 0:1],
                                    None, ALU.mult).then_inc(bo4_ready, 1)
            dve.wait_ge(rstd1_ready, 2)
            dve.wait_ge(consts, CONSTS)

            def pair(j):
                if isinstance(j, int) and j == 2:
                    empty_group(LATER)
                if runs(j, lag=1):
                    residual(dve, j - 1, 0)
                if runs(j, lag=3):
                    own_rank(dve, j - 3)
                if runs(j, lag=1):
                    residual_stats(dve, j - 1, 0)
                if runs(j, lag=3):
                    sum_exps(dve, j - 3)
                if runs(j, ahead=1) and not (isinstance(j, int) and j == 1):
                    head_max(dve, j + 1, 0)
                if runs(j, lag=3):
                    gate(dve, j - 3)
                    send_payload(dve, j - 3, 0)
                if runs(j, lag=2):
                    copy_x2T(dve, j - 2)
                invert_sums(dve, j, 1)
                if runs(j, ahead=2):
                    normalise_x(dve, j + 2)
                if runs(j, lag=1):
                    residual(dve, j - 1, 1)
                if runs(j, lag=3):
                    send_payload(dve, j - 3, 1)
                if runs(j, lag=2):
                    max_logit(dve, j - 2)
                if runs(j, lag=1):
                    residual_stats(dve, j - 1, 1)
                if runs(j, lag=2):
                    subtract_max(dve, j - 2)
                if runs(j, lag=1):
                    aggregate_x2(dve, j - 1)
                if runs(j, lag=2):
                    mark_maxima(dve, j - 2)
                if runs(j, ahead=1):
                    head_max(dve, j + 1, 1)
                if runs(j, lag=2):
                    first_maximum(dve, j - 2)
                if not (isinstance(j, int) and j < 1) and runs(j, ahead=1):
                    invert_sums(dve, j + 1, 0)
                if runs(j, lag=2):
                    mark_expert(dve, j - 2)
                if runs(j, ahead=2):
                    copy_xT(dve, j + 2)
                if isinstance(j, int) and j < 1:
                    for g in range(LATE, LATER):
                        empty_group(g)
                        if g == LATE + 1:
                            invert_sums(dve, j + 1, 0)
                        if g == LATER - 2:
                            head_max(dve, j + 2, 0)
                if runs(j, lag=2):
                    count_tokens(dve, j - 2, 0)
                    count_tokens(dve, j - 2, 1)
                if runs(j, lag=1, ahead=1):
                    normalise_x2(dve, j - 1)

            pairs(dve, pair)
            r = NPAIR - 1
            residual(dve, r, 0)
            normalise_x2(dve, r - 1)
            own_rank(dve, r - 2)
            residual_stats(dve, r, 0)
            sum_exps(dve, r - 2)
            gate(dve, r - 2)
            for i in range(2):
                send_payload(dve, r - 2, i, SPARE)
            residual(dve, r, 1)
            copy_x2T(dve, r - 1)
            residual_stats(dve, r, 1)
            aggregate_x2(dve, r)
            max_logit(dve, r - 1)
            subtract_max(dve, r - 1)
            mark_maxima(dve, r - 1)
            normalise_x2(dve, r)
            first_maximum(dve, r - 1)
            mark_expert(dve, r - 1)
            count_tokens(dve, r - 1, 0)
            count_tokens(dve, r - 1, 1)
            copy_x2T(dve, r)
            sum_exps(dve, r - 1)
            gate(dve, r - 1)
            own_rank(dve, r - 1, PT0)
            send_payload(dve, r - 1, 0)
            max_logit(dve, r)
            send_payload(dve, r - 1, 1)
            subtract_max(dve, r)
            mark_maxima(dve, r)
            first_maximum(dve, r)
            mark_expert(dve, r)
            count_tokens(dve, r, 0)
            count_tokens(dve, r, 1)
            sum_exps(dve, r)
            own_rank(dve, r)
            gate(dve, r)
            send_payload(dve, r, 0, LAST)

            steps = [0]

            def plan(step):
                step.then_inc(plan_step, 1)
                steps[0] += 1

            def need():
                dve.wait_ge(plan_step, steps[0])

            dve.wait_ge(cnt_ready, 1)
            plan(nc.vector.tensor_tensor(above[:, :, :], bank[:, PT1, 0:E].unsqueeze(2).to_broadcast([P, E, T]),
                                         tile_edge[:, :].unsqueeze(1).to_broadcast([P, E, T]), ALU.is_gt))
            plan(nc.vector.tensor_copy(cnt[:, :], bank[:, PT1, 0:E]))
            send_payload(dve, r, 1, LAST)
            need()
            plan(nc.vector.reduce_sum(ntiles[:, :], above[:, :, :], AX))
            plan(nc.vector.tensor_copy(deltas[:, 0, :], ones8[:, 0:E - 1]))
            plan(nc.vector.tensor_tensor(deltas[:, 2, :], cnt[:, 1:E], cnt[:, 0:E - 1], ALU.subtract))
            need()
            plan(nc.vector.tensor_tensor_scan(cum_in[:, :], ones8[:, :], ntiles[:, :], 0.0, ALU.mult, ALU.add))
            plan(nc.vector.tensor_scalar(deltas[:, 1, :], ntiles[:, 0:E - 1], float(P), None, ALU.mult))
            plan(nc.vector.tensor_scalar(first_free[:, :], cnt[:, 0:1], float(-P), None, ALU.add))
            need()
            plan(nc.vector.tensor_tensor(passed[:, :, :], tile_no[:, :].unsqueeze(2).to_broadcast([P, NJ, E - 1]),
                                         cum_in[:, 0:E - 1].unsqueeze(1).to_broadcast([P, NJ, E - 1]), ALU.is_ge))
            need()
            plan(nc.vector.tensor_tensor(picked[:, :, :, :], passed[:, :, :].unsqueeze(1).to_broadcast([P, 3, NJ, E - 1]),
                                         deltas[:, :, :].unsqueeze(2).to_broadcast([P, 3, NJ, E - 1]), ALU.mult))
            need()
            plan(nc.vector.reduce_sum(pick[:, :, :], picked[:, :, :, :], AX))
            need()
            expert, first_row, count_change = pick[:, 0, :], pick[:, 1, :], pick[:, 2, :]
            plan(nc.vector.tensor_scalar(where_i[:, 1, :], expert, float(P), None, ALU.mult))
            assert steps[0] == EXPERTS_PLANNED
            plan(nc.vector.tensor_scalar(last_start[:, :], count_change, first_free[:, :], 0.0, ALU.add, ALU.max))
            plan(nc.vector.tensor_tensor(wanted[:, :], tile_row[:, :], first_row, ALU.subtract))
            need()
            plan(nc.vector.tensor_tensor(start[:, :], wanted[:, :], last_start[:, :], ALU.min))
            need()
            plan(nc.vector.scalar_tensor_tensor(where_i[:, 0, :], expert, float(REGION), start[:, :], ALU.mult, ALU.add))
            assert steps[0] == ROWS_PLANNED
            plan(nc.vector.tensor_scalar(w2_at_i[:, :], expert, float(FC * D), None, ALU.mult))
            plan(nc.vector.tensor_scalar(b2_at_i[:, :], expert, float(D), None, ALU.mult))
            plan(nc.vector.tensor_tensor(low[:, :], wanted[:, :], start[:, :], ALU.subtract))
            plan(nc.vector.scalar_tensor_tensor(high[:, :], count_change, cnt[:, 0:1], start[:, :], ALU.add, ALU.subtract))
            need()
            plan(nc.vector.tensor_scalar(not_below[:, :], low[:, :], part_no[:, :], None, ALU.is_le))
            need()
            plan(nc.vector.scalar_tensor_tensor(own[:, :], high[:, :], part_no[:, :], not_below[:, :], ALU.is_gt, ALU.mult))
            need()
            plan(nc.vector.tensor_scalar(drop[:, :], own[:, :], -DROP, DROP, ALU.mult, ALU.add))
            need()
            assert steps[0] == PLAN_STEPS

            def normalise_rows(k, uses):
                dve.wait_ge(erows_in[k], 16 * uses)
                if not (k < 2 and isinstance(uses, int) and uses < 2):
                    dve.wait_ge(exT_psum[(k - 2) % NW], uses - (k < 2))
                nc.vector.tensor_scalar(exn[:, k % 2, :], erows[:, k, 0:D], erows[:, k, MEAN:MEAN + 1], erows[:, k, RSTD:RSTD + 1],
                                        ALU.subtract, ALU.mult).then_inc(exn_ready[k], 1)

            def add_b1(k, uses):
                dve.wait_ge(h_ready[k], uses)
                if not (k < 2 and isinstance(uses, int) and uses < 2):
                    dve.wait_ge(hid_ready[(k - 2) % NW], uses - (k < 2))
                nc.vector.tensor_tensor(hbias[:, k % 2, :, :], bank[:, 2 + k % 2, :].rearrange("p (c k) -> p c k", c=FC),
                                        w1_sb[:, k, F:F + FC].unsqueeze(2).to_broadcast([P, FC, P]),
                                        ALU.add).then_inc(hbias_ready[k], 1)

            def finish(j, k, uses, b2_at):
                if not (isinstance(uses, int) and uses < 2):
                    dve.wait_ge(stored[k], 16 * (uses - 1))
                nc.vector.tensor_scalar(token_i[:, k:k + 1], erows[:, k, TOKEN:TOKEN + 1], drop[:, bass.ds(j, 1)], None,
                                        ALU.add)
                dve.wait_ge(y_ready[k], uses)
                nc.vector.scalar_tensor_tensor(ybias[:, k % 2, :], bank[:, 4 + k % 2, 0:D], tg[:, 1:2],
                                               b2_bc[:, bass.ds(b2_at, D)], ALU.mult, ALU.add).then_inc(ybias_ready[k], 1)
                dve.wait_ge(ybias_ready[k], uses)
                nc.vector.scalar_tensor_tensor(eout[:, k, :], ybias[:, k % 2, :], erows[:, k, GATE:GATE + 1], erows[:, k, 0:D],
                                               ALU.mult, ALU.add).then_inc(eout_ready[k], 1)

            def slot(j, k, q, b2_at):
                whole = not isinstance(j, int)
                if whole or j >= 1:
                    finish(j - 1, (k - 1) % NW, q + 1 - (k < 1), b2_at)
                if whole or j + 3 < NJ:
                    normalise_rows((k + 3) % NW, q + 1 + (k + 3) // NW)
                if whole or j + 1 < NJ:
                    add_b1((k + 1) % NW, q + 1 + (k + 1) // NW)

            dve.wait_ge(b2_scaled, 1)
            for k in range(3):
                normalise_rows(k, 1)
            add_b1(0, 1)
            slots(dve, slot, b2_at_i, lag=1)
            _, (b2_at,) = nc.values_load_multi_w_load_instructions(
                b2_at_i[0:1, NJ - 1:NJ], engines=[dve.engine], min_val=0, max_val=(E - 1) * D,
                skip_runtime_bounds_check_because=BOUNDED)
            finish(NJ - 1, (NJ - 1) % NW, (NJ - 1) // NW + 1, b2_at)


EXPERTS_PLANNED = 12
ROWS_PLANNED = 16
PLAN_STEPS = 23
CONSTS = 14


_INS = ['x', 'ctx_t', 'g_xattn', 'g_ffn', 'Wq_t', 'Wk_t', 'Wv_t', 'L0_xattn_Wo', 'L0_xattn_bo',
        'L0_ffn_Wr', 'W1b1', 'L0_ffn_W2', 'L0_ffn_b2']
_OUTS = [((4, 512, 128), 'float32')]


def kernel(**inputs):
    import numpy as _np
    import concourse.bacc as _bacc
    from concourse import mybir as _mybir
    from concourse.bass_utils import run_bass_kernel_spmd as _run

    b1 = _np.asarray(inputs['L0_ffn_b1'])
    laid = dict(inputs)
    laid['ctx_t'] = _np.asarray(inputs['ctx_768']).transpose(2, 0, 1)
    for name in ('Wq', 'Wk', 'Wv'):
        laid[name + '_t'] = _np.asarray(inputs['L0_xattn_' + name]).T
    laid['W1b1'] = _np.concatenate(
        [_np.asarray(inputs['L0_ffn_W1']), b1.reshape(b1.shape[0], -1, 128).transpose(0, 2, 1)], axis=2)

    nc = _bacc.Bacc("TRN2", target_bir_lowering=False, num_devices=1)
    arrays, args = {}, []
    for name in _INS:
        a = _np.ascontiguousarray(laid[name])
        arrays[f"in_{name}_dram"] = a
        args.append(nc.dram_tensor(f"in_{name}_dram", a.shape, _mybir.dt.from_np(a.dtype), kind="ExternalInput").ap())
    for i, (shape, dtype) in enumerate(_OUTS):
        dt = _mybir.dt.from_np(_np.dtype(dtype))
        args.append(nc.dram_tensor(f"out_{i}_dram", shape, dt, kind="ExternalOutput").ap())
    flamingo_block(nc, *args)
    r = _run(nc, [arrays], core_ids=[0])
    got = tuple(r.results[0][f"out_{i}_dram"] for i in range(len(_OUTS)))
    return got[0]
```
